# Optimizing a Trainium2 kernel written in Bass

```python
import numpy as np
import jax
import jax.numpy as jnp

def _softmax(x, axis=-1):
    return jax.nn.softmax(x, axis=axis)

def _gelu(x):
    return jax.nn.gelu(x, approximate=True)

def _silu(x):
    return jax.nn.silu(x)

def _sigmoid(x):
    return jax.nn.sigmoid(x)

def _layernorm(x, axis=-1, eps=1e-05):
    m = jnp.mean(x, axis=axis, keepdims=True)
    v = jnp.var(x, axis=axis, keepdims=True)
    return (x - m) / jnp.sqrt(v + eps)

def _scatter_add(tgt, idx, src, axis=0):
    return tgt.at[idx].add(src)

def _segment_sum(src, seg, n):
    return jax.ops.segment_sum(src, seg, n)
kernel_name = 'mk_gnn_resnorm_d1_gnn_r32_6561de'

def setup_inputs(seed: int=0):
    np.random.seed(seed)
    _w = jnp.asarray

    def _rec_inputs():
        import jax
        import jax.numpy as jnp
        _gk = jax.random.key(seed)
        x = -8.776e-05 + 1 * jax.random.normal(jax.random.fold_in(_gk, 1), (10000, 512), jnp.float32)
        src = jax.random.randint(jax.random.fold_in(_gk, 2), (10000,), 0, 10000, jnp.int32)
        dst = jnp.minimum((10000 * jax.random.uniform(jax.random.fold_in(_gk, 3), (10000,)) ** 2.0).astype(jnp.int32), 9999)
        _o = jnp.argsort(dst, stable=True)
        src = src[_o]
        dst = dst[_o]
        edge_attr_512 = 2.93046e-05 + 1.00006 * jax.random.normal(jax.random.fold_in(_gk, 11), (10000, 512), jnp.float32)
        return (x, src, dst, edge_attr_512)
    x, src, dst, edge_attr_512 = _rec_inputs()

    def _L0_gnn_setup():
        import jax, jax.numpy as jnp
        import numpy as np
        N, E, D = (10000, 5000, 512)
        BN_EPS = 1e-05
        key = jax.random.key(seed)
        k = jax.random.split(key, 6)
        x = jax.random.normal(k[0], (N, D), dtype=jnp.float32)
        edge_index = jax.random.randint(k[1], (2, E), 0, N, dtype=jnp.int32)
        edge_attr = jax.random.normal(k[2], (E, D), dtype=jnp.float32)
        W1 = jax.random.normal(k[3], (D, D), dtype=jnp.float32) * 0.02
        b1 = jnp.zeros((D,), dtype=jnp.float32)
        W2 = jax.random.normal(k[4], (D, D), dtype=jnp.float32) * 0.02
        b2 = jnp.zeros((D,), dtype=jnp.float32)
        gamma = jnp.ones((D,), dtype=jnp.float32)
        beta = jnp.zeros((D,), dtype=jnp.float32)
        return {'x': x, 'edge_index': edge_index, 'edge_attr': edge_attr, 'W1': W1, 'b1': b1, 'W2': W2, 'b2': b2, 'gamma': gamma, 'beta': beta}
    _L0_gnn_all = _L0_gnn_setup()
    _L0_gnn_in = {k: v for k, v in _L0_gnn_all.items() if k in ('W1', 'b1', 'W2', 'b2', 'gamma', 'beta')}
    del _L0_gnn_all
    return {'x': x, 'src': src, 'dst': dst, 'edge_attr_512': edge_attr_512, 'L0_gnn_W1': _L0_gnn_in['W1'], 'L0_gnn_b1': _L0_gnn_in['b1'], 'L0_gnn_W2': _L0_gnn_in['W2'], 'L0_gnn_b2': _L0_gnn_in['b2'], 'L0_gnn_gamma': _L0_gnn_in['gamma'], 'L0_gnn_beta': _L0_gnn_in['beta']}

def reference(x, src, dst, edge_attr_512, L0_gnn_W1, L0_gnn_b1, L0_gnn_W2, L0_gnn_b2, L0_gnn_gamma, L0_gnn_beta):
    import jax
    import jax.numpy as jnp

    def _L0_gnn_ref(x, edge_index, edge_attr, W1, b1, W2, b2, gamma, beta):
        import jax, jax.numpy as jnp
        import numpy as np
        N, E, D = (10000, 5000, 512)
        BN_EPS = 1e-05
        src, dst = (edge_index[0], edge_index[1])
        msg = jax.nn.relu(x[src] + edge_attr)
        agg = jax.ops.segment_sum(msg, dst, num_segments=x.shape[0])
        h = x + agg
        h = jax.nn.relu(h @ W1 + b1) @ W2 + b2
        h = x + h
        mean = h.mean(axis=0)
        var = h.var(axis=0)
        h = (h - mean) * jax.lax.rsqrt(var + BN_EPS) * gamma + beta
        return h
    edge_index = jnp.stack([src, dst])
    x = _layernorm(x + _L0_gnn_ref(x, edge_index, edge_attr_512, L0_gnn_W1, L0_gnn_b1, L0_gnn_W2, L0_gnn_b2, L0_gnn_gamma, L0_gnn_beta), axis=-1)
    return x

_drawn_inputs = setup_inputs


def setup_inputs(seed=0):
    import zlib

    import numpy as np

    out = dict(_drawn_inputs(seed))
    spreads = {'L0_gnn_b1': (0.0, 0.736),
     'L0_gnn_b2': (0.0, 0.8),
     'L0_gnn_gamma': (1.0, 0.2),
     'L0_gnn_beta': (0.0, 0.1)}
    factors = {}
    for name, (base, spread) in spreads.items():
        noise = np.random.default_rng([zlib.crc32(name.encode()), seed]).standard_normal(out[name].shape)
        drawn = base * np.exp(spread * noise) if base else spread * noise
        out[name] = jnp.asarray(drawn.astype(out[name].dtype))
    for name, factor in factors.items():
        out[name] = (out[name] * factor).astype(out[name].dtype)
    return out
```

```python
from contextlib import ExitStack

import concourse.bass as bass
from concourse import mybir
from concourse.alu_op_type import AluOpType as ALU

P = 128
F32 = mybir.dt.float32
F32R = mybir.dt.float32r
I32 = mybir.dt.int32
ACT = mybir.ActivationFunctionType
AX_X = mybir.AxisListType.X

BN_EPS = 1e-5
LN_EPS = 1e-5
FAR = 1024



def gnn_resnorm(nc, x, src, dst, edge, w1, b1, w2, b2, gamma, beta, out):
    N, D = x.shape
    E = src.shape[0]
    KB = D // P
    PAIR = 2 * P
    PAIRS = N // PAIR
    REST = N - PAIRS * PAIR
    TILES = 2 * PAIRS + 1
    GRAN = P // 2
    CH_A = -(-E // P)
    CH_B = CH_A - 1
    LAST_ROW = E - P
    TN = 80
    SPILLED = 14
    LOOPED = PAIRS - 1
    KEPT = LOOPED - SPILLED
    assert 0 < REST <= P and REST % 2 == 0 and TILES <= TN and CH_A <= P
    assert SPILLED % 2 == 0 and KEPT % 2 == 0 and KEPT > SPILLED
    TAIL_A = E - (CH_A - 1) * P
    LAST_GRAN = (E - 1) // GRAN
    assert TAIL_A <= GRAN and CH_A * P - E >= GRAN
    TAIL_B = E - GRAN - (CH_B - 1) * P
    RING = 4
    TRING = 4

    h2_dram = nc.dram_tensor("h2_spilled", [SPILLED * PAIR, D], F32, kind="Internal").ap()

    with ExitStack() as ctx:
        def sb(name, shape, dt=F32):
            return ctx.enter_context(nc.sbuf_tensor(name, shape, dt))

        def pb(name, shape):
            return ctx.enter_context(nc.psum_tensor(name, shape, F32))

        def sem(name):
            return ctx.enter_context(nc.semaphore(name))

        store = sb("store", [P, 2 * (KEPT + 1) + 1, D])
        ident = sb("ident", [P, P])
        ones = sb("ones", [P, P])
        acc1 = sb("acc1", [P, D])
        acc2 = sb("acc2", [P, D])
        bn_a = sb("bn_a", [P, D])
        iota_row = sb("iota_row", [P, P])
        tile_off = sb("tile_off", [P, TN])
        dst_col = sb("dst_col", [P, CH_A + CH_B])
        src_col = sb("src_col", [P, CH_A + CH_B], I32)
        idx = [sb(f"idx{s}", [P, 1], I32) for s in range(2)]
        table = sb("table", [1, 4, TN], I32)
        b1_col = sb("b1_col", [P, KB])
        main = ExitStack()

        def sbm(name, shape, dt=F32):
            return main.enter_context(nc.sbuf_tensor(name, shape, dt))

        w_hi = [sbm(f"w{i}_hi", [P, KB, D], F32R) for i in (1, 2)]
        w_lo = [sbm(f"w{i}_lo", [P, KB, D], F32R) for i in (1, 2)]
        hT_hi = sbm("hT_hi", [P, KB, PAIR], F32R)
        hT_lo = sbm("hT_lo", [P, KB, PAIR], F32R)
        zT_hi = sbm("zT_hi", [P, KB, PAIR], F32R)
        zT_lo = sbm("zT_lo", [P, KB, PAIR], F32R)
        z_full = sbm("z_full", [P, 2, PAIR])
        x_in = sbm("x_in", [P, 2, 2, D])
        h = sbm("h", [P, 2, D])
        e_in = sbm("e_in", [P, 2, D])
        g_in = [sbm(f"g_in{s}", [P, D]) for s in range(2)]
        m_hi = sbm("m_hi", [P, RING, D], F32R)
        m_lo = sbm("m_lo", [P, RING, D], F32R)
        onehot = sbm("onehot", [P, RING, P], F32R)
        sq = sbm("sq", [P, 2, D])
        b2_all = sbm("b2_all", [P, D])
        w_raw = store[:, 0:2 * KB, :].rearrange("p (i k) d -> p i k d", i=2)
        st = [2 * KB]

        def scratch(parts, cols, dt=F32):
            view = store[0:parts, st[0], 0:cols]
            st[0] += 1
            return view if dt == F32 else view.bitcast(dt)

        dst_a, dst_b, src_a, src_b = (scratch(n, P, I32) for n in (CH_A, CH_B, CH_A, CH_B))
        dst_af, dst_bf, src_af, src_bf = (scratch(n, P) for n in (CH_A, CH_B, CH_A, CH_B))
        tile_i = scratch(CH_A, P, I32)
        tile_f = scratch(CH_A, P)
        tile_up = scratch(CH_A, P)
        t_max = scratch(CH_A, 2)
        t_min = scratch(CH_A, 2)
        gran = scratch(CH_A, 2)
        gran_up = scratch(CH_A, 2)
        gran_last = scratch(CH_A, 2)
        gran_first = scratch(CH_A, 2)
        iota_n = scratch(P, TN)
        above = scratch(P, TN)
        cover = [scratch(CH_A, TN) for _ in range(2)]
        part_f = [scratch(CH_A, TN) for _ in range(2)]
        part_l = [scratch(CH_A, TN) for _ in range(2)]
        range_f = scratch(CH_A, TN)
        range_l = scratch(CH_A, TN)
        nf = scratch(TN, 16)
        ni = scratch(TN, 16, I32)
        upper = scratch(TN, TN)
        assert st[0] <= 2 * (KEPT + 1) + 1
        main.close()

        def sbt(name, shape, dt=F32):
            return ctx.enter_context(nc.sbuf_tensor(name, shape, dt))

        x_tail = sbt("x_tail", [P, TRING, 2, D])
        u_out = sbt("u_out", [P, TRING, 2, D])
        stats = sbt("stats", [P, 2, 2, 6])
        mean_var = sbt("mean_var", [P, 2, 2, 2])
        std = sbt("std", [P, TRING, 2])
        rstd = sbt("rstd", [P, TRING, 2])
        shift = sbt("shift", [P, TRING, 2])
        c_parts = sbt("c_parts", [64, D], F32R)
        c_pick = sbt("c_pick", [64, P], F32R)
        bn_c = sbt("bn_c", [P, D])
        gamma_all = sbt("gamma_all", [P, D])
        beta_all = sbt("beta_all", [P, D])
        bn_mean = sbt("bn_mean", [P, D])
        bn_sq = sbt("bn_sq", [P, D])
        bn_var = sbt("bn_var", [P, D])
        bn_std = sbt("bn_std", [P, D])
        bn_rstd = sbt("bn_rstd", [P, D])
        bn_ma = sbt("bn_ma", [P, D])
        eps_bn = sbt("eps_bn", [P, 1])
        eps_ln = sbt("eps_ln", [P, 1])

        ps_sum = [pb(f"ps_sum{a}", [P, D]) for a in range(2)]
        ps_turn = [pb(f"ps_turn{a}", [P, KB, P]) for a in range(2)]
        ps_z = [pb(f"ps_z{a}", [P, D]) for a in range(2)]
        ps_o = [pb(f"ps_o{a}", [P, D]) for a in range(2)]
        tail_banks = [[ps_sum[0], ps_sum[1]], [ps_o[0], ps_o[1]]]

        s_idx = sem("s_idx")
        s_fill = sem("s_fill")
        s_w = sem("s_w")
        s_bias = sem("s_bias")
        s_const = sem("s_const")
        s_set = sem("s_set")
        s_link = sem("s_link")
        s_turned = sem("s_turned")
        s_table = sem("s_table")
        s_cols = sem("s_cols")
        s_acc0 = sem("s_acc0")
        s_wsplit = sem("s_wsplit")
        s_wlow = sem("s_wlow")
        e_landed = [sem(f"e_landed{s}") for s in range(2)]
        g_landed = [sem(f"g_landed{s}") for s in range(2)]
        idx_copied = sem("idx_copied")
        m_summed = sem("m_summed")
        m_hi_done = sem("m_hi_done")
        m_done = sem("m_done")
        m_used = sem("m_used")
        x_landed = sem("x_landed")
        h_done = sem("h_done")
        h_turned = sem("h_turned")
        hT_hi_done = sem("hT_hi_done")
        hT_done = sem("hT_done")
        z_ready = sem("z_ready")
        z_read = sem("z_read")
        z_done = sem("z_done")
        o_ready = sem("o_ready")
        xb_done = sem("xb_done")
        h2_done = sem("h2_done")
        sq_done = sem("sq_done")
        acc1_done = sem("acc1_done")
        acc_done = sem("acc_done")
        spilled = sem("spilled")
        s_gb = sem("s_gb")
        s_tot = sem("s_tot")
        s_bn = sem("s_bn")
        s_bn_act = sem("s_bn_act")
        s_eps = sem("s_eps")
        xt_landed = [sem(f"xt_landed{s}") for s in range(2)]
        back_landed = [sem(f"back_landed{s}") for s in range(2)]
        out_landed = [sem(f"out_landed{s}") for s in range(2)]
        pre_ready = sem("pre_ready")
        scaled = sem("scaled")
        u_done = sem("u_done")
        u_self = sem("u_self")
        stat_self = sem("stat_self")
        var_done = sem("var_done")
        std_done = sem("std_done")
        rstd_done = sem("rstd_done")
        shift_done = sem("shift_done")
        norm_done = sem("norm_done")

        block = ctx.enter_context(nc.Block())

        def by_slot(eng, step, do):
            with eng.If(step % 2 == 0):
                do(0)
            with eng.Else():
                do(1)

        def look_up(eng, n, row, low, high):
            return eng.value_load(table[0:1, row, bass.ds(n, 1)], min_val=low, max_val=high)

        MOST = CH_A
        STEPS = MOST * TILES

        def first_row(eng, n): return look_up(eng, n, 0, 0, E)
        def first_col(eng, n): return look_up(eng, n, 1, 0, CH_A + CH_B - 1)
        def chunks(eng, n): return look_up(eng, n, 2, 1, MOST)
        def steps_before(eng, n): return look_up(eng, n, 3, 0, STEPS)

        def rows_of(array, pair):
            return rows_from(array, pair * PAIR)

        def rows_from(array, start):
            rows = array[start:start + PAIR, :] if isinstance(start, int) else array[bass.ds(start, PAIR), :]
            return rows.rearrange("(a p) d -> p a d", p=P)

        def pick(buf, slot, rows=P):
            if isinstance(slot, int):
                return buf[0:rows, slot]
            view = buf[0:rows, bass.ds(slot, 1)]
            rest = " ".join("abc"[:len(view.shape) - 2])
            return view.rearrange(f"p o {rest} -> p (o {rest[0]}) {rest[1:]}")

        @block.sync
        def _(sp):
            sp.wait_ge(s_fill, 1)
            sp.dma_start(dst_a[0:CH_A - 1, :], dst[0:(CH_A - 1) * P].rearrange("(c p) -> c p", p=P)).then_inc(s_idx, 16)
            sp.dma_start(dst_a[CH_A - 1:CH_A, P - TAIL_A:P], dst[E - TAIL_A:E].rearrange("(c p) -> c p", c=1)).then_inc(s_idx, 16)
            sp.dma_start(dst_b[0:CH_B - 1, :], dst[GRAN:GRAN + (CH_B - 1) * P].rearrange("(c p) -> c p", p=P)).then_inc(s_idx, 16)
            sp.dma_start(dst_b[CH_B - 1:CH_B, P - TAIL_B:P], dst[E - TAIL_B:E].rearrange("(c p) -> c p", c=1)).then_inc(s_idx, 16)
            sp.dma_start(src_a[0:CH_A - 1, :], src[0:(CH_A - 1) * P].rearrange("(c p) -> c p", p=P)).then_inc(s_idx, 16)
            sp.dma_start(src_a[CH_A - 1:CH_A, :], src[LAST_ROW:E].rearrange("(c p) -> c p", c=1)).then_inc(s_idx, 16)
            sp.dma_start(src_b[0:CH_B - 1, :], src[GRAN:GRAN + (CH_B - 1) * P].rearrange("(c p) -> c p", p=P)).then_inc(s_idx, 16)
            sp.dma_start(src_b[CH_B - 1:CH_B, :], src[LAST_ROW:E].rearrange("(c p) -> c p", c=1)).then_inc(s_idx, 16)
            sp.dma_start(w_raw[:, 0], w1.rearrange("(k p) d -> p k d", p=P)).then_inc(s_w, 16)
            sp.dma_start(w_raw[:, 1], w2.rearrange("(k p) d -> p k d", p=P)).then_inc(s_w, 16)
            sp.wait_ge(s_table, 1)
            with sp.Fori(0, TILES) as n:
                row0, count, before = first_row(sp, n), chunks(sp, n), steps_before(sp, n)
                with sp.Fori(0, count) as k:
                    step = before + k
                    row = row0 + k * P
                    over = row > LAST_ROW
                    row = (row - over * (row - LAST_ROW)).with_bounds(min_val=0, max_val=LAST_ROW)

                    row = sp.snap(row)
                    parts_made = sp.snap(step + 1)

                    def load(s):
                        sp.wait_ge(m_done, parts_made)
                        sp.dma_start(e_in[:, s, :], edge[bass.ds(row, P), :]).then_inc(e_landed[s], 16)
                    by_slot(sp, step, load)

            for par in range(2):
                sp.wait_ge(norm_done, par + 1)
                sp.dma_start(rows_of(out, par + KEPT), u_out[:, par, :, :]).then_inc(out_landed[par], 16)
                sp.wait_ge(u_done, par + 3)
                sp.dma_start(store[:, 2 * par:2 * par + 2, :], rows_of(h2_dram, par)).then_inc(back_landed[par], 16)
            def wait_for(semaphore, value):
                sp.wait_ge(s_bn, 8)
                sp.wait_ge(semaphore, value)

            with sp.Fori(1, SPILLED // 2) as j:
                for par in range(2):
                    q = j * 2 + par
                    start, before = sp.snap((q + KEPT) * PAIR), sp.snap(j * 16)
                    wait_for(out_landed[par], before)
                    wait_for(norm_done, q + 1)
                    sp.dma_start(rows_from(out, start), pick(u_out, q % TRING)).then_inc(out_landed[par], 16)
                    start = sp.snap(q * PAIR)
                    wait_for(u_done, q + 3)
                    wait_for(back_landed[par], before)
                    sp.dma_start(store[:, bass.ds(2 * q, 2), :], rows_from(h2_dram, start)).then_inc(back_landed[par], 16)

            def finish(lo, hi, shift_rows):
                with sp.Fori(lo, hi) as j:
                    for par in range(2):
                        q = j * 2 + par
                        start, before = sp.snap((q - shift_rows) * PAIR), sp.snap(j * 16)
                        wait_for(out_landed[par], before)
                        wait_for(norm_done, q + 1)
                        sp.dma_start(rows_from(out, start), pick(u_out, q % TRING)).then_inc(out_landed[par], 16)
            finish(SPILLED // 2, KEPT // 2, 0)
            finish(KEPT // 2, LOOPED // 2, KEPT)
            sp.wait_ge(norm_done, LOOPED + 1)
            sp.wait_ge(out_landed[0], 16 * (LOOPED // 2))
            sp.dma_start(rows_of(out, PAIRS - 1), u_out[:, LOOPED % TRING, :, :]).then_inc(out_landed[0], 16)
            sp.wait_ge(norm_done, LOOPED + 2)
            sp.wait_ge(out_landed[1], 16 * (LOOPED // 2))
            sp.dma_start(out[N - REST:N, :], u_out[0:REST, (LOOPED + 1) % TRING, 0, :]).then_inc(out_landed[1], 16)
            for par in range(2):
                sp.wait_ge(out_landed[par], 16 * (LOOPED // 2 + 1))

        @block.gpsimd
        def _(pool):
            nc.gpsimd.memset(dst_a, -1)
            nc.gpsimd.memset(dst_b, -1).then_inc(s_fill, 1)
            nc.gpsimd.memset(ones[:], 1.0).then_inc(s_const, 1)
            pool.wait_ge(s_const, 1)
            nc.gpsimd.affine_select(out=ident[:], in_=ones[:], compare_op=ALU.is_equal, fill=0.0, base=0,
                                    pattern=[[1, P]], channel_multiplier=-1)
            nc.gpsimd.affine_select(out=upper, in_=ones[0:TN, 0:TN], compare_op=ALU.is_gt, fill=0.0, base=0,
                                    pattern=[[1, TN]], channel_multiplier=-1)
            nc.gpsimd.iota(iota_row[:], pattern=[[1, P]], base=0, channel_multiplier=0,
                           allow_small_or_imprecise_dtypes=True)
            nc.gpsimd.iota(iota_n, pattern=[[1, TN]], base=0, channel_multiplier=0,
                           allow_small_or_imprecise_dtypes=True)
            nc.gpsimd.iota(tile_off[:], pattern=[[P, TN]], base=0, channel_multiplier=0,
                           allow_small_or_imprecise_dtypes=True)
            nc.gpsimd.iota(gran, pattern=[[1, 2]], base=0, channel_multiplier=2,
                           allow_small_or_imprecise_dtypes=True).then_inc(s_const, 1)
            nc.gpsimd.memset(acc1[:], 0.0)
            nc.gpsimd.memset(acc2[:], 0.0).then_inc(s_acc0, 1)
            pool.wait_ge(s_acc0, 1)

            def gathers(n):
                col0, count, before = first_col(pool, n), chunks(pool, n), steps_before(pool, n)
                with pool.Fori(0, count) as k:
                    step = before + k
                    pool.wait_ge(m_summed, step + 1)

                    def gather(s):
                        nc.gpsimd.tensor_copy(idx[s][:], src_col[:, bass.ds((col0 + k).with_bounds(min_val=0, max_val=CH_A + CH_B - 1), 1)]).then_inc(idx_copied, 1)
                        pool.wait_ge(s_cols, 1)
                        pool.wait_ge(idx_copied, step + 1)
                        nc.gpsimd.indirect_dma_start(
                            out=g_in[s][:], out_offset=None, in_=x,
                            in_offset=bass.IndirectOffsetOnAxis(ap=idx[s][:, 0:1], axis=0),
                        ).then_inc(g_landed[s], 16)
                    by_slot(pool, step, gather)

            def add_b2(i, slot):
                pool.wait_ge(h_done, 2 * i + 4)
                for a in range(2):
                    xa = x_in[:, slot, a, :]
                    last = nc.gpsimd.tensor_tensor(xa, xa, b2_all[:], ALU.add)
                last.then_inc(xb_done, 1)

            def add_up(n, a, slot, rows):
                pool.wait_ge(h2_done, n + 3)
                h2 = pick(store, slot, rows)
                pool.wait_ge(acc1_done, n + 1)
                nc.gpsimd.tensor_tensor(acc1[0:rows, :], acc1[0:rows, :], h2, ALU.add).then_inc(acc1_done, 1)
                pool.wait_ge(sq_done, n + 1)
                pool.wait_ge(acc_done, n + 2)
                nc.gpsimd.tensor_tensor(acc2[0:rows, :], acc2[0:rows, :], sq[0:rows, a, :], ALU.add).then_inc(acc_done, 1)

            pool.sem_inc(acc1_done, 1)
            pool.sem_inc(acc_done, 2)
            pool.wait_ge(s_table, 1)
            pool.wait_ge(s_cols, 1)
            gathers(0)
            gathers(1)
            gathers(2)
            gathers(3)
            pool.wait_ge(s_bias, 32)
            add_b2(0, 0)
            gathers(4)
            gathers(5)

            def body(i, slot_before):
                add_b2(i, i % 2)
                for a in range(2):
                    add_up(2 * i - 2 + a, a, slot_before + a, P)
                gathers(2 * i + 4)
                gathers(2 * i + 5)
            with pool.Fori(1, KEPT + 1) as i:
                body(i, 2 * i - 2)
            with pool.Fori(KEPT + 1, PAIRS - 2) as i:
                body(i, 2 * i - 2 - 2 * KEPT)
            i = PAIRS - 2
            add_b2(i, i % 2)
            for a in range(2):
                add_up(2 * i - 2 + a, a, 2 * i - 2 - 2 * KEPT + a, P)
            gathers(TILES - 1)
            i = PAIRS - 1
            add_b2(i, i % 2)
            for a in range(2):
                add_up(2 * i - 2 + a, a, 2 * i - 2 - 2 * KEPT + a, P)
            pool.wait_ge(h_done, TILES + 2)
            xa = x_in[0:REST, PAIRS % 2, 0, :]
            nc.gpsimd.tensor_tensor(xa, xa, b2_all[0:REST, :], ALU.add).then_inc(xb_done, 1)
            for a in range(2):
                add_up(2 * PAIRS - 2 + a, a, 2 * KEPT + a, P)
            add_up(TILES - 1, 0, 2 * KEPT + 2, REST)

            pool.wait_ge(s_bn, 6)

            def scale(slot):
                for a in range(2):
                    s = slot + a
                    h2 = pick(store, s)
                    last = nc.gpsimd.tensor_tensor(h2, h2, bn_a[:], ALU.mult)
                last.then_inc(scaled, 1)
            with pool.Fori(0, KEPT) as q:
                scale(2 * q)
            with pool.Fori(0, SPILLED // 2) as j:
                for par in range(2):
                    pool.wait_ge(back_landed[par], j * 16 + 16)
                    scale(4 * j + 2 * par)
            scale(2 * KEPT)
            h2 = store[0:REST, 2 * KEPT + 2, :]
            nc.gpsimd.tensor_tensor(h2, h2, bn_a[0:REST, :], ALU.mult).then_inc(scaled, 1)

        @block.scalar
        def _(act):
            act.dma_start(b1_col[:], b1.rearrange("(k p) -> p k", p=P), allow_slow_non_contiguous=True).then_inc(s_bias, 16)
            act.dma_start(b2_all[:], b2.rearrange("(o d) -> o d", o=1).broadcast_to([P, D])).then_inc(s_bias, 16)
            act.sem_inc(z_read, 2)
            act.wait_ge(s_w, 32)
            for w in range(2):
                nc.scalar.copy(w_hi[w][:], w_raw[:, w]).then_inc(s_wsplit, 1)

            def load_x(i, slot):
                act.dma_start(pick(x_in, slot), rows_of(x, i)).then_inc(x_landed, 16)

            act.dma_start(x_in[:, 0, :, :], rows_of(x, 0)).then_inc(x_landed, 16)
            act.wait_ge(x_landed, 16)
            act.dma_start(x_in[:, 1, :, :], rows_of(x, 1)).then_inc(x_landed, 16)

            def hT_high(n, a, rows):
                act.wait_ge(h_turned, n + 3)
                nc.scalar.copy(hT_hi[:, :, a * P:a * P + rows], ps_turn[a][:, :, 0:rows]).then_inc(hT_hi_done, 1)

            def z_high(i, cols):
                for f in range(KB):
                    act.wait_ge(z_ready, 4 * i + f + 1)
                    act.wait_ge(z_done, 4 * i + f + 1)
                    nc.scalar.activation(z_full[:, f % 2, 0:cols], ps_z[f % 2][:, 0:cols], ACT.Relu, bias=b1_col[:, f:f + 1])
                    nc.scalar.activation(zT_hi[:, f, 0:cols], ps_z[f % 2][:, 0:cols], ACT.Relu, bias=b1_col[:, f:f + 1]).then_inc(z_read, 1)

            def squares(n, a, slot, rows):
                act.wait_ge(h2_done, n + 3)
                act.wait_ge(acc_done, n + 1)
                h2 = pick(store, slot, rows)
                nc.scalar.activation(sq[0:rows, a, :], h2, ACT.Square).then_inc(sq_done, 1)

            act.wait_ge(s_bias, 32)
            for a in range(2):
                hT_high(a, a, P)

            def body(i, slot, spill):
                z_high(i, PAIR)
                for a in range(2):
                    hT_high(2 * i + 2 + a, a, P)
                for a in range(2):
                    squares(2 * i + a, a, slot + a, P)
                load_x(i + 2, i % 2)
                if spill:
                    act.dma_start(rows_of(h2_dram, i), store[:, bass.ds(slot, 2), :]).then_inc(spilled, 16)
            with act.Fori(0, SPILLED) as i:
                body(i, 2 * i, True)
            with act.Fori(SPILLED, KEPT) as i:
                body(i, 2 * i, False)
            with act.Fori(KEPT, LOOPED - 1) as i:
                body(i, 2 * i - 2 * KEPT, False)
            i = LOOPED - 1
            z_high(i, PAIR)
            for a in range(2):
                hT_high(2 * i + 2 + a, a, P)
            for a in range(2):
                squares(2 * i + a, a, 2 * i - 2 * KEPT + a, P)
            act.dma_start(x_in[0:REST, PAIRS % 2, 0, :], x[N - REST:N, :]).then_inc(x_landed, 16)
            i = PAIRS - 1
            z_high(i, PAIR)
            hT_high(2 * i + 2, 0, REST)
            for a in range(2):
                squares(2 * i + a, a, 2 * KEPT + a, P)
            z_high(PAIRS, REST)
            squares(TILES - 1, 0, 2 * KEPT + 2, REST)

            def load_tail(q, pair, par):
                act.dma_start(pick(x_tail, q % TRING), rows_of(x, pair)).then_inc(xt_landed[par], 16)

            act.wait_ge(acc_done, TILES + 2)
            act.wait_ge(o_ready, TILES)
            act.dma_start(gamma_all[:], gamma.rearrange("(o d) -> o d", o=1).broadcast_to([P, D])).then_inc(s_gb, 16)
            act.dma_start(beta_all[:], beta.rearrange("(o d) -> o d", o=1).broadcast_to([P, D])).then_inc(s_gb, 16)
            load_tail(0, KEPT, 0)
            load_tail(1, KEPT + 1, 1)
            act.wait_ge(s_tot, 1)
            nc.scalar.mul(bn_mean[:], ps_z[0][:], 1.0 / N).then_inc(s_bn_act, 1)
            act.wait_ge(s_tot, 2)
            nc.scalar.mul(bn_sq[:], ps_z[1][:], 1.0 / N).then_inc(s_bn_act, 1)
            act.wait_ge(s_bn, 2)
            nc.scalar.activation(bn_std[:], bn_var[:], ACT.Sqrt, bias=eps_bn[:]).then_inc(s_bn_act, 1)

            def root(q, slot, par, rows, tiles):
                act.wait_ge(var_done, q + 1)
                nc.scalar.activation(pick(std, slot, rows)[:, 0:tiles], mean_var[0:rows, par, 0:tiles, 1], ACT.Sqrt, bias=eps_ln[0:rows, :]).then_inc(std_done, 1)

            def norm(q, slot, rows, tiles):
                act.wait_ge(shift_done, q + 1)
                for a in range(tiles):
                    u = pick(u_out, slot, rows)[:, a, :]
                    last = nc.scalar.activation(u, u, ACT.Identity, bias=pick(shift, slot, rows)[:, a:a + 1], scale=pick(rstd, slot, rows)[:, a:a + 1])
                last.then_inc(norm_done, 1)

            def tail_body(q, j, par, pair_ahead):
                if pair_ahead is not None:
                    act.wait_ge(pre_ready, q + 1)
                    act.wait_ge(xt_landed[par], j * 16 + 16)
                    load_tail(q + 2, pair_ahead, par)
                root(q, q % TRING, par, P, 2)
                norm(q - 1, (q + TRING - 1) % TRING, P, 2)

            act.wait_ge(xt_landed[0], 16)
            load_tail(2, KEPT + 2, 0)
            root(0, 0, 0, P, 2)
            act.wait_ge(xt_landed[1], 16)
            load_tail(3, KEPT + 3, 1)
            root(1, 1, 1, P, 2)
            norm(0, 0, P, 2)
            for lo, hi, pair_shift in ((1, SPILLED // 2 - 1, KEPT), (SPILLED // 2 - 1, KEPT // 2 - 1, 0),
                                       (KEPT // 2 - 1, LOOPED // 2 - 1, -KEPT)):
                with act.Fori(lo, hi) as j:
                    for par in range(2):
                        q = 2 * j + par
                        tail_body(q, j, par, q + 2 + pair_shift)
            j = LOOPED // 2 - 1
            q = 2 * j
            act.wait_ge(pre_ready, q + 1)
            act.wait_ge(xt_landed[0], 16 * (j + 1))
            load_tail(q + 2, PAIRS - 1, 0)
            root(q, q % TRING, 0, P, 2)
            norm(q - 1, (q - 1) % TRING, P, 2)
            act.wait_ge(pre_ready, q + 2)
            act.wait_ge(xt_landed[1], 16 * (j + 1))
            act.dma_start(x_tail[0:REST, (q + 3) % TRING, 0, :], x[N - REST:N, :]).then_inc(xt_landed[1], 16)
            root(q + 1, (q + 1) % TRING, 1, P, 2)
            norm(q, q % TRING, P, 2)
            root(LOOPED, LOOPED % TRING, 0, P, 2)
            norm(LOOPED - 1, (LOOPED - 1) % TRING, P, 2)
            root(LOOPED + 1, (LOOPED + 1) % TRING, 1, REST, 1)
            norm(LOOPED, LOOPED % TRING, P, 2)
            norm(LOOPED + 1, (LOOPED + 1) % TRING, REST, 1)

        @block.tensor
        def _(pe):
            mm = nc.tensor.matmul
            pe.sem_inc(m_used, RING)
            pe.sem_inc(h_turned, 2)
            pe.sem_inc(pre_ready, 2)
            pe.wait_ge(s_const, 2)
            pe.wait_ge(s_set, 1)
            cols = ps_turn[0][:, :, :]
            nc.tensor.transpose(ps_turn[0][:, 0, 0:CH_A], dst_af, ident[0:CH_A, 0:CH_A])
            nc.tensor.transpose(ps_turn[0][:, 1, 0:CH_B], dst_bf, ident[0:CH_B, 0:CH_B])
            nc.tensor.transpose(ps_turn[0][:, 2, 0:CH_A], src_af, ident[0:CH_A, 0:CH_A])
            nc.tensor.transpose(ps_turn[0][:, 3, 0:CH_B], src_bf, ident[0:CH_B, 0:CH_B]).then_inc(s_turned, 1)
            pe.wait_ge(s_set, 2)
            nc.tensor.transpose(ps_turn[1][0:TN, 0, 0:CH_A], range_f, ident[0:CH_A, 0:CH_A])
            nc.tensor.transpose(ps_turn[1][0:TN, 1, 0:CH_A], range_l, ident[0:CH_A, 0:CH_A]).then_inc(s_turned, 1)
            pe.wait_ge(s_set, 3)
            mm(ps_z[0][0:1, 0:TN], nf[:, 8:9], ident[0:TN, 0:TN], start=True, stop=True)
            mm(ps_z[0][0:1, TN:2 * TN], nf[:, 9:10], ident[0:TN, 0:TN], start=True, stop=True)
            mm(ps_z[0][0:1, 2 * TN:3 * TN], nf[:, 10:11], ident[0:TN, 0:TN], start=True, stop=True)
            mm(ps_z[0][0:1, 3 * TN:4 * TN], nf[:, 10:11], upper, start=True, stop=True).then_inc(s_turned, 1)
            pe.wait_ge(s_table, 1)

            def edge_sums(n, a):
                count, before = chunks(pe, n), steps_before(pe, n)
                pe.wait_ge(h_done, n + 1)

                def one(step, start):
                    pe.wait_ge(m_done, step + 3)

                    def use(s):
                        mm(ps_sum[a][:], onehot[:, s, :], m_hi[:, s, :], start=start, stop=False, skip_group_check=True)
                        mm(ps_sum[a][:], onehot[:, s, :], m_lo[:, s, :], start=False, stop=True,
                           skip_group_check=True).then_inc(m_used, 1)
                    with pe.If(step % 4 <= 1):
                        with pe.If(step % 4 == 0):
                            use(0)
                        with pe.Else():
                            use(1)
                    with pe.Else():
                        with pe.If(step % 4 == 2):
                            use(2)
                        with pe.Else():
                            use(3)
                one(before, True)
                with pe.If(count > 1):
                    with pe.Fori(1, count) as k:
                        one(before + k, False)
                with pe.Else():
                    pe.nop()

            def turn(n, a, rows):
                pe.wait_ge(h_done, n + 3)
                pe.wait_ge(hT_done, n + 1)
                for k in range(KB):
                    t = nc.tensor.transpose(ps_turn[a][:, k, 0:rows], h[0:rows, a, k * P:(k + 1) * P], ident[0:rows, 0:rows])
                t.then_inc(h_turned, 1)

            def layer1(i, cols, tiles_done):
                pe.wait_ge(hT_done, tiles_done + 2)
                for f in range(KB):
                    pe.wait_ge(z_read, 4 * i + f + 1)
                    out_ = ps_z[f % 2][:, 0:cols]
                    parts = [(w_hi[0], hT_hi), (w_lo[0], hT_hi), (w_hi[0], hT_lo)]
                    for m in range(3 * KB):
                        w, r = parts[m // KB]
                        t = mm(out_, w[:, m % KB, f * P:(f + 1) * P], r[:, m % KB, 0:cols], start=(m == 0), stop=(m == 3 * KB - 1))
                    t.then_inc(z_ready, 1)

            def layer2(i, n, a):
                pe.wait_ge(h2_done, n + 1)
                for f in range(KB):
                    pe.wait_ge(z_done, 4 * i + f + 3)
                    for m, (l, w) in enumerate(((zT_hi, w_hi[1]), (zT_hi, w_lo[1]), (zT_lo, w_hi[1]))):
                        t = mm(ps_o[a][:], l[:, f, a * P:(a + 1) * P], w[:, f, :], start=(f == 0 and m == 0), stop=(f == KB - 1 and m == 2))
                t.then_inc(o_ready, 1)

            pe.wait_ge(s_wlow, 2)
            for a in range(2):
                edge_sums(a, a)
            for a in range(2):
                turn(a, a, P)
            with pe.Fori(0, LOOPED) as i:
                layer1(i, PAIR, 2 * i + 2)
                for a in range(2):
                    edge_sums(2 * i + 2 + a, a)
                layer2(i, 2 * i, 0)
                for a in range(2):
                    turn(2 * i + 2 + a, a, P)
                layer2(i, 2 * i + 1, 1)
            i = PAIRS - 1
            layer1(i, PAIR, 2 * i + 2)
            edge_sums(TILES - 1, 0)
            layer2(i, 2 * i, 0)
            turn(TILES - 1, 0, REST)
            layer2(i, 2 * i + 1, 1)
            layer1(PAIRS, REST, TILES)
            layer2(PAIRS, TILES - 1, 0)

            pe.wait_ge(acc_done, TILES + 2)
            mm(ps_z[0][:], ones[:], acc1[:], start=True, stop=True).then_inc(s_tot, 1)
            mm(ps_z[1][:], ones[:], acc2[:], start=True, stop=True).then_inc(s_tot, 1)

            def pre(q, slot, par, rows, tiles):
                pe.wait_ge(u_done, q + 1)
                for a in range(tiles):
                    bank = tail_banks[par][a]
                    mm(bank[:], c_pick[:], c_parts[:], start=True, stop=False, skip_group_check=True)
                    t = mm(bank[0:rows, :] if rows == P else bank[:], ident[:] if rows == P else ident[0:rows, :],
                           pick(x_tail, slot, rows)[:, a, :], start=False, stop=True, skip_group_check=True)
                t.then_inc(pre_ready, 1)
            pe.wait_ge(s_bn, 8)
            with pe.Fori(0, LOOPED // 2) as j:
                for par in range(2):
                    q = j * 2 + par
                    pe.wait_ge(xt_landed[par], j * 16 + 16)
                    pre(q, q % TRING, par, P, 2)
            pe.wait_ge(xt_landed[0], 16 * (LOOPED // 2 + 1))
            pre(LOOPED, LOOPED % TRING, 0, P, 2)
            pe.wait_ge(xt_landed[1], 16 * (LOOPED // 2 + 1))
            pre(LOOPED + 1, (LOOPED + 1) % TRING, 1, REST, 1)

        @block.vector
        def _(dve):
            v = nc.vector
            dve.sem_inc(m_summed, 2)
            dve.sem_inc(m_done, 2)
            dve.sem_inc(h_done, 2)
            dve.sem_inc(hT_done, 2)
            dve.sem_inc(z_done, 2)
            dve.sem_inc(h2_done, 2)
            dve.sem_inc(u_done, 2)
            chain = [0]
            def link(ins):
                chain[0] += 1
                ins.then_inc(s_link, 1)
                dve.wait_ge(s_link, chain[0])

            dve.wait_ge(s_idx, 16 * 8)
            v.tensor_copy(dst_af, dst_a)
            v.tensor_copy(dst_bf, dst_b)
            v.tensor_copy(src_af, src_a)
            v.tensor_copy(src_bf, src_b).then_inc(s_set, 1)
            link(v.tensor_scalar(tile_i, dst_a, 7, None, ALU.arith_shift_right))
            link(v.tensor_copy(tile_f, tile_i))
            link(v.tensor_scalar(tile_up, tile_f, 0.0, float(FAR), ALU.is_lt, ALU.mult))
            link(v.tensor_tensor(tile_up, tile_up, tile_f, ALU.add))
            v.tensor_reduce(t_max, tile_f.rearrange("c (g e) -> c g e", g=2), AX_X, ALU.max)
            link(v.tensor_reduce(t_min, tile_up.rearrange("c (g e) -> c g e", g=2), AX_X, ALU.min))
            dve.wait_ge(s_const, 2)
            link(v.tensor_scalar(gran_up, gran, float(LAST_GRAN), None, ALU.min))
            v.tensor_scalar(gran_last, gran_up, 1.0, None, ALU.add)
            link(v.tensor_scalar(gran_first, gran_up, -1.0, float(FAR), ALU.mult, ALU.add))
            for g in range(2):
                v.tensor_scalar(above[0:CH_A, :] if g == 0 else cover[1], iota_n[0:CH_A, :], t_min[:, g:g + 1], None, ALU.is_ge)
            link(v.tensor_scalar(part_f[0], iota_n[0:CH_A, :], t_max[:, 0:1], None, ALU.is_le))
            link(v.tensor_scalar(part_f[1], iota_n[0:CH_A, :], t_max[:, 1:2], None, ALU.is_le))
            link(v.tensor_tensor(cover[0], above[0:CH_A, :], part_f[0], ALU.mult))
            link(v.tensor_tensor(cover[1], cover[1], part_f[1], ALU.mult))
            for g in range(2):
                v.tensor_scalar(part_f[g], cover[g], gran_first[:, g:g + 1], None, ALU.mult)
                link(v.tensor_scalar(part_l[g], cover[g], gran_last[:, g:g + 1], None, ALU.mult))
            v.tensor_tensor(range_f, part_f[0], part_f[1], ALU.max)
            v.tensor_tensor(range_l, part_l[0], part_l[1], ALU.max).then_inc(s_set, 1)
            dve.wait_ge(s_turned, 1)
            v.tensor_copy(dst_col[:, 0:CH_A], ps_turn[0][:, 0, 0:CH_A])
            v.tensor_copy(dst_col[:, CH_A:CH_A + CH_B], ps_turn[0][:, 1, 0:CH_B])
            v.tensor_copy(src_col[:, 0:CH_A], ps_turn[0][:, 2, 0:CH_A])
            v.tensor_copy(src_col[:, CH_A:CH_A + CH_B], ps_turn[0][:, 3, 0:CH_B]).then_inc(s_cols, 1)
            dve.wait_ge(s_turned, 2)
            v.tensor_reduce(nf[:, 0:1], ps_turn[1][0:TN, 0, 0:CH_A], AX_X, ALU.max)
            link(v.tensor_reduce(nf[:, 1:2], ps_turn[1][0:TN, 1, 0:CH_A], AX_X, ALU.max))
            v.tensor_scalar(nf[:, 2:3], nf[:, 1:2], 1.0, None, ALU.is_ge)
            v.tensor_scalar(nf[:, 3:4], nf[:, 0:1], -1.0, float(FAR), ALU.mult, ALU.add)
            link(v.tensor_scalar(nf[:, 4:5], nf[:, 1:2], -1.0, 0.0, ALU.add, ALU.max))
            link(v.tensor_tensor(nf[:, 5:6], nf[:, 3:4], nf[:, 2:3], ALU.mult))
            link(v.tensor_tensor(nf[:, 6:7], nf[:, 4:5], nf[:, 5:6], ALU.subtract))
            v.tensor_copy(ni[:, 0:1], nf[:, 6:7])
            link(v.tensor_copy(ni[:, 1:2], nf[:, 5:6]))
            v.tensor_scalar(ni[:, 2:4], ni[:, 0:2], 1, None, ALU.arith_shift_right)
            link(v.tensor_scalar(ni[:, 4:5], ni[:, 1:2], 1, None, ALU.bitwise_and))
            link(v.tensor_copy(nf[:, 11:14], ni[:, 2:5]))
            v.tensor_scalar(nf[:, 8:9], nf[:, 5:6], float(GRAN), None, ALU.mult)
            v.tensor_scalar(nf[:, 10:11], nf[:, 11:12], 1.0, None, ALU.add)
            v.scalar_tensor_tensor(nf[:, 9:10], nf[:, 13:14], float(CH_A), nf[:, 12:13], ALU.mult, ALU.add).then_inc(s_set, 1)
            dve.wait_ge(s_turned, 3)
            v.tensor_copy(table[0:1, :, :].rearrange("o r n -> o (r n)"), ps_z[0][0:1, 0:4 * TN]).then_inc(s_table, 1)
            for w in range(2):
                dve.wait_ge(s_wsplit, w + 1)
                v.tensor_tensor(w_lo[w][:], w_raw[:, w], w_hi[w][:].bitcast(F32), ALU.subtract).then_inc(s_wlow, 1)
            dve.wait_ge(s_wlow, 2)

            def steps(n):
                col0, count, before = first_col(dve, n), chunks(dve, n), steps_before(dve, n)
                with dve.Fori(0, count) as k:
                    step = before + k
                    par = step % 2
                    slot = step % RING

                    def add(s):
                        nth = step // 2
                        dve.wait_ge(e_landed[s], nth * 16 + 16)
                        dve.wait_ge(g_landed[s], nth * 16 + 16)
                        v.tensor_tensor(e_in[:, s, :], e_in[:, s, :], g_in[s][:], ALU.add).then_inc(m_summed, 1)
                    by_slot(dve, step, add)
                    dve.wait_ge(m_used, step + 1)
                    v.tensor_scalar(pick(onehot, slot), iota_row[:], tile_off[:, bass.ds(n, 1)],
                                    dst_col[:, bass.ds((col0 + k).with_bounds(min_val=0, max_val=CH_A + CH_B - 1), 1)], ALU.add, ALU.is_equal)
                    dve.wait_ge(m_summed, step + 3)
                    e = pick(e_in, par)
                    hi = pick(m_hi, slot)
                    v.tensor_scalar(hi, e, 0.0, None, ALU.max).then_inc(m_hi_done, 1)
                    dve.wait_ge(m_hi_done, step + 1)
                    v.scalar_tensor_tensor(pick(m_lo, slot), e, 0.0, hi.bitcast(F32), ALU.max, ALU.subtract).then_inc(m_done, 1)

            def make_h(n, a, i, slot, rows):
                count, before = chunks(dve, n), steps_before(dve, n)
                dve.wait_ge(m_used, before + count + RING)
                dve.wait_ge(x_landed, 16 * i + 16)
                dve.wait_ge(h_turned, n + 1)
                v.tensor_tensor(h[0:rows, a, :], ps_sum[a][0:rows, :], pick(x_in, slot, rows)[:, a, :], ALU.add).then_inc(h_done, 1)

            def hT_low(n, a, rows):
                dve.wait_ge(hT_hi_done, n + 1)
                v.tensor_tensor(hT_lo[:, :, a * P:a * P + rows], ps_turn[a][:, :, 0:rows],
                                hT_hi[:, :, a * P:a * P + rows].bitcast(F32), ALU.subtract).then_inc(hT_done, 1)

            def z_low(i, f, cols):
                dve.wait_ge(z_read, 4 * i + f + 3)
                v.tensor_tensor(zT_lo[:, f, 0:cols], z_full[:, f % 2, 0:cols], zT_hi[:, f, 0:cols].bitcast(F32), ALU.subtract).then_inc(z_done, 1)

            def make_h2(n, a, i, slot, xslot, rows):
                dve.wait_ge(o_ready, n + 1)
                dve.wait_ge(xb_done, i + 1)
                h2 = pick(store, slot, rows)
                v.tensor_tensor(h2, ps_o[a][0:rows, :], pick(x_in, xslot, rows)[:, a, :], ALU.add).then_inc(h2_done, 1)

            for a in range(2):
                steps(a)
            for a in range(2):
                make_h(a, a, 0, 0, P)
            for a in range(2):
                hT_low(a, a, P)

            def body(i, slot):
                z_low(i, 0, PAIR)
                z_low(i, 1, PAIR)
                for a in range(2):
                    steps(2 * i + 2 + a)
                z_low(i, 2, PAIR)
                z_low(i, 3, PAIR)
                for a in range(2):
                    make_h(2 * i + 2 + a, a, i + 1, (i + 1) % 2, P)
                make_h2(2 * i, 0, i, slot, i % 2, P)
                for a in range(2):
                    hT_low(2 * i + 2 + a, a, P)
                make_h2(2 * i + 1, 1, i, slot + 1, i % 2, P)
            with dve.Fori(0, KEPT) as i:
                body(i, 2 * i)
            dve.wait_ge(spilled, 16 * SPILLED)
            with dve.Fori(KEPT, LOOPED) as i:
                body(i, 2 * i - 2 * KEPT)
            i = PAIRS - 1
            for f in range(2):
                z_low(i, f, PAIR)
            steps(TILES - 1)
            for f in range(2, KB):
                z_low(i, f, PAIR)
            make_h(TILES - 1, 0, PAIRS, PAIRS % 2, REST)
            make_h2(2 * i, 0, i, 2 * KEPT, i % 2, P)
            hT_low(TILES - 1, 0, REST)
            make_h2(2 * i + 1, 1, i, 2 * KEPT + 1, i % 2, P)
            for f in range(KB):
                z_low(PAIRS, f, REST)
            make_h2(TILES - 1, 0, PAIRS, 2 * KEPT + 2, PAIRS % 2, REST)

            dve.wait_ge(o_ready, TILES)
            dve.wait_ge(acc_done, TILES + 2)
            v.memset(eps_bn[:], BN_EPS)
            v.memset(eps_ln[:], LN_EPS)
            v.memset(c_pick[:].bitcast(F32), 0.0).then_inc(s_eps, 1)
            dve.wait_ge(s_eps, 1)
            v.memset(c_pick[0:1, :].bitcast(F32), 1.0)
            v.memset(c_pick[32:33, :].bitcast(F32), 1.0).then_inc(s_eps, 1)
            dve.wait_ge(s_bn_act, 2)
            v.tensor_tensor(bn_var[:], bn_mean[:], bn_mean[:], ALU.mult).then_inc(s_bn, 1)
            dve.wait_ge(s_bn, 1)
            v.tensor_tensor(bn_var[:], bn_sq[:], bn_var[:], ALU.subtract).then_inc(s_bn, 1)
            dve.wait_ge(s_bn_act, 3)
            v.reciprocal(bn_rstd[:], bn_std[:]).then_inc(s_bn, 1)
            dve.wait_ge(s_bn, 3)
            dve.wait_ge(s_gb, 32)
            v.tensor_tensor(bn_a[:], bn_rstd[:], gamma_all[:], ALU.mult).then_inc(s_bn, 1)
            dve.wait_ge(s_bn, 4)
            v.tensor_tensor(bn_ma[:], bn_mean[:], bn_a[:], ALU.mult).then_inc(s_bn, 1)
            dve.wait_ge(s_bn, 5)
            v.tensor_tensor(bn_c[:], beta_all[:], bn_ma[:], ALU.subtract).then_inc(s_bn, 1)
            dve.wait_ge(s_bn, 6)
            v.tensor_copy(c_parts[0:64, :], bn_c[0:64, :]).then_inc(s_bn, 1)
            dve.wait_ge(s_bn, 7)
            v.tensor_tensor(c_parts[32:64, :], bn_c[32:64, :], c_parts[32:64, :].bitcast(F32), ALU.subtract).then_inc(s_bn, 1)

            def pair_stats(q, slot, par, store_slot, rows, tiles):
                dve.wait_ge(pre_ready, q + 3)
                dve.wait_ge(scaled, q + 1)
                for a in range(tiles):
                    s = store_slot + a
                    t = pick(store, s, rows)
                    last = v.tensor_tensor(pick(u_out, slot, rows)[:, a, :], tail_banks[par][a][0:rows, :], t, ALU.add)
                last.then_inc(u_done, 1)
                dve.wait_ge(s_bn, 8)
                dve.wait_ge(u_done, q + 3)
                for a in range(tiles):
                    st_ = stats[0:rows, par, a, :]
                    last = v.bn_stats(st_, pick(u_out, slot, rows)[:, a, :])
                last.then_inc(stat_self, 1)
                dve.wait_ge(s_bn, 8)
                dve.wait_ge(stat_self, q + 1)
                for a in range(tiles):
                    st_ = stats[0:rows, par, a, :]
                    mv = mean_var[0:rows, par, a, :]
                    last = v.bn_aggr(mv, st_)
                last.then_inc(var_done, 1)

            def scale_shift(q, slot, par, rows, tiles):
                dve.wait_ge(std_done, q + 1)
                v.reciprocal(pick(rstd, slot, rows)[:, 0:tiles], pick(std, slot, rows)[:, 0:tiles]).then_inc(rstd_done, 1)
                dve.wait_ge(rstd_done, q + 1)
                v.scalar_tensor_tensor(pick(shift, slot, rows)[:, 0:tiles], mean_var[0:rows, par, 0:tiles, 0], -1.0,
                                       pick(rstd, slot, rows)[:, 0:tiles], ALU.mult, ALU.mult).then_inc(shift_done, 1)

            pair_stats(0, 0, 0, 0, P, 2)
            pair_stats(1, 1, 1, 2, P, 2)
            scale_shift(0, 0, 0, P, 2)
            for q in (2, 3):
                pair_stats(q, q, q % 2, 2 * q, P, 2)
                scale_shift(q - 1, q - 1, (q - 1) % 2, P, 2)
            for lo, hi, shift_slots in ((2, KEPT // 2, 0), (KEPT // 2, LOOPED // 2, KEPT)):
                with dve.Fori(lo, hi) as j:
                    for par in range(2):
                        q = j * 2 + par
                        dve.wait_ge(out_landed[par], j * 16 - 16)
                        pair_stats(q, q % TRING, par, 2 * q - 2 * shift_slots, P, 2)
                        scale_shift(q - 1, (q + TRING - 1) % TRING, 1 - par, P, 2)
            for q, slot, rows, tiles in ((LOOPED, 2 * KEPT, P, 2), (LOOPED + 1, 2 * KEPT + 2, REST, 1)):
                dve.wait_ge(out_landed[q % 2], 16 * (q // 2 - 1))
                pair_stats(q, q % TRING, q % 2, slot, rows, tiles)
                scale_shift(q - 1, (q - 1) % TRING, (q - 1) % 2, P, 2)
            scale_shift(LOOPED + 1, (LOOPED + 1) % TRING, 1, REST, 1)


_INS = ['x', 'src', 'dst', 'edge_attr_512', 'L0_gnn_W1', 'L0_gnn_b1', 'L0_gnn_W2', 'L0_gnn_b2', 'L0_gnn_gamma', 'L0_gnn_beta']
_OUTS = [((10000, 512), 'float32')]


def kernel(**inputs):
    import numpy as _np
    import concourse.bacc as _bacc
    from concourse import mybir as _mybir
    from concourse.bass_utils import run_bass_kernel_spmd as _run

    nc = _bacc.Bacc("TRN2", target_bir_lowering=False, num_devices=1)
    arrays, args = {}, []
    for name in _INS:
        a = _np.ascontiguousarray(inputs[name])
        arrays[f"in_{name}_dram"] = a
        args.append(nc.dram_tensor(f"in_{name}_dram", a.shape, _mybir.dt.from_np(a.dtype), kind="ExternalInput").ap())
    for i, (shape, dtype) in enumerate(_OUTS):
        dt = _mybir.dt.from_np(_np.dtype(dtype))
        args.append(nc.dram_tensor(f"out_{i}_dram", shape, dt, kind="ExternalOutput").ap())
    gnn_resnorm(nc, *args)
    r = _run(nc, [arrays], core_ids=[0])
    got = tuple(r.results[0][f"out_{i}_dram"] for i in range(len(_OUTS)))
    return got[0]
```

```python
from contextlib import ExitStack

import concourse.bass as bass
from concourse import mybir
from concourse.alu_op_type import AluOpType as ALU

P = 128
F32 = mybir.dt.float32
F32R = mybir.dt.float32r
I32 = mybir.dt.int32
ACT = mybir.ActivationFunctionType
AX_X = mybir.AxisListType.X

BN_EPS = 1e-5
LN_EPS = 1e-5
FAR = 1024



def gnn_resnorm(nc, x, src, dst, edge, w1, b1, w2, b2, gamma, beta, out):
    N, D = x.shape
    E = src.shape[0]
    KB = D // P
    PAIR = 2 * P
    PAIRS = N // PAIR
    REST = N - PAIRS * PAIR
    TILES = 2 * PAIRS + 1
    GRAN = P // 2
    CH_A = -(-E // P)
    CH_B = CH_A - 1
    LAST_ROW = E - P
    TN = 80
    SPILLED = 16
    LOOPED = PAIRS - 1
    KEPT = LOOPED - SPILLED
    assert 0 < REST <= P and REST % 2 == 0 and TILES <= TN and CH_A <= P
    assert SPILLED % 2 == 0 and KEPT % 2 == 0 and KEPT > SPILLED
    TAIL_A = E - (CH_A - 1) * P
    LAST_GRAN = (E - 1) // GRAN
    assert TAIL_A <= GRAN and CH_A * P - E >= GRAN
    TAIL_B = E - GRAN - (CH_B - 1) * P
    STEPS_PER_TILE = 2
    ROUND = 2 * STEPS_PER_TILE
    ERING = 2 * ROUND
    NOTHING = CH_A + CH_B
    TP = TN // 2
    TPR = TP + 8
    TRING = 4

    h2_dram = nc.dram_tensor("h2_spilled", [SPILLED * PAIR, D], F32, kind="Internal").ap()

    with ExitStack() as ctx:
        def sb(name, shape, dt=F32):
            return ctx.enter_context(nc.sbuf_tensor(name, shape, dt))

        def pb(name, shape):
            return ctx.enter_context(nc.psum_tensor(name, shape, F32))

        def sem(name):
            return ctx.enter_context(nc.semaphore(name))

        store = sb("store", [P, 2 * (KEPT + 1) + 1, D])
        ident = sb("ident", [P, P])
        ones = sb("ones", [P, P])
        acc1 = sb("acc1", [P, D])
        acc2 = sb("acc2", [P, D])
        iota_row = sb("iota_row", [P, P])
        tile_off = sb("tile_off", [P, TN])
        dst_col = sb("dst_col", [P, NOTHING + 1])
        src_col = sb("src_col", [P, NOTHING + 1], I32)
        idx = [sb(f"idx{s}", [P, 1], I32) for s in range(ERING)]
        rel = sb("rel", [P, ERING])
        table = sb("table", [1, 4, TN], I32)
        b1_col = sb("b1_col", [P, KB])
        row_parts = sb("row_parts", [64, D], F32R)
        row_pick = sb("row_pick", [64, P], F32R)
        main = ExitStack()

        def sbm(name, shape, dt=F32):
            return main.enter_context(nc.sbuf_tensor(name, shape, dt))

        w_hi = [sbm(f"w{i}_hi", [P, KB, D], F32R) for i in (1, 2)]
        w_lo = [sbm(f"w{i}_lo", [P, KB, D], F32R) for i in (1, 2)]
        hT_hi = sbm("hT_hi", [P, KB, PAIR], F32R)
        hT_lo = sbm("hT_lo", [P, KB, PAIR], F32R)
        zT_hi = sbm("zT_hi", [P, KB, PAIR], F32R)
        zT_lo = sbm("zT_lo", [P, KB, PAIR], F32R)
        z_full = sbm("z_full", [P, 2, PAIR])
        x_in = sbm("x_in", [P, 2, 2, D])
        h = sbm("h", [P, 2, D])
        mess = sbm("mess", [P, ERING, D])
        m_hi = sbm("m_hi", [P, ROUND, D], F32R)
        m_lo = sbm("m_lo", [P, ROUND, D], F32R)
        onehot = sbm("onehot", [P, ROUND, P], F32R)
        sq = sbm("sq", [P, 2, D])
        w_raw = store[:, 0:2 * KB, :].rearrange("p (i k) d -> p i k d", i=2)
        st = [2 * KB]

        def scratch(parts, cols, dt=F32):
            view = store[0:parts, st[0], 0:cols]
            st[0] += 1
            return view if dt == F32 else view.bitcast(dt)

        dst_a, dst_b, src_a, src_b = (scratch(n, P, I32) for n in (CH_A, CH_B, CH_A, CH_B))
        dst_af, dst_bf, src_af, src_bf = (scratch(n, P) for n in (CH_A, CH_B, CH_A, CH_B))
        b2_all = scratch(64, D)
        tile_i = scratch(CH_A, P, I32)
        tile_f = scratch(CH_A, P)
        tile_up = scratch(CH_A, P)
        t_max = scratch(CH_A, 2)
        t_min = scratch(CH_A, 2)
        gran = scratch(CH_A, 2)
        gran_up = scratch(CH_A, 2)
        gran_last = scratch(CH_A, 2)
        gran_first = scratch(CH_A, 2)
        iota_n = scratch(P, TN)
        above = scratch(P, TN)
        cover = [scratch(CH_A, TN) for _ in range(2)]
        part_f = [scratch(CH_A, TN) for _ in range(2)]
        part_l = [scratch(CH_A, TN) for _ in range(2)]
        range_f = scratch(CH_A, TN)
        range_l = scratch(CH_A, TN)
        nf = scratch(TN, 16)
        ni = scratch(TN, 16, I32)
        upper = scratch(TP, TPR)
        most = scratch(1, TP)
        rounds_i = scratch(1, TP, I32)
        rounds_half = scratch(1, TP, I32)
        rounds_up = scratch(1, TP)
        rounds_f = scratch(1, TP)
        rounds_col = scratch(TP, 1)
        assert st[0] <= 2 * (KEPT + 1) + 1
        main.close()

        def sbt(name, shape, dt=F32):
            return ctx.enter_context(nc.sbuf_tensor(name, shape, dt))

        x_tail = sbt("x_tail", [P, TRING, 2, D])
        u_out = sbt("u_out", [P, TRING, 2, D])
        stats = sbt("stats", [P, 2, 2, 6])
        mean_var = sbt("mean_var", [P, 2, 2, 2])
        std = sbt("std", [P, TRING, 2])
        rstd = sbt("rstd", [P, TRING, 2])
        shift = sbt("shift", [P, TRING, 2])
        bn_a = sbt("bn_a", [P, D])
        bn_c = sbt("bn_c", [P, D])
        gamma_all = sbt("gamma_all", [P, D])
        beta_all = sbt("beta_all", [P, D])
        bn_mean = sbt("bn_mean", [P, D])
        bn_sq = sbt("bn_sq", [P, D])
        bn_var = sbt("bn_var", [P, D])
        bn_std = sbt("bn_std", [P, D])
        bn_rstd = sbt("bn_rstd", [P, D])
        bn_ma = sbt("bn_ma", [P, D])
        eps_bn = sbt("eps_bn", [P, 1])
        eps_ln = sbt("eps_ln", [P, 1])

        ps_sum = [pb(f"ps_sum{a}", [P, D]) for a in range(2)]
        ps_turn = [pb(f"ps_turn{a}", [P, KB, P]) for a in range(2)]
        ps_z = [pb(f"ps_z{a}", [P, D]) for a in range(2)]
        ps_o = [pb(f"ps_o{a}", [P, D]) for a in range(2)]
        tail_banks = [[ps_sum[0], ps_sum[1]], [ps_o[0], ps_o[1]]]

        s_idx = sem("s_idx")
        s_fill = sem("s_fill")
        s_w = sem("s_w")
        s_bias = sem("s_bias")
        s_const = sem("s_const")
        s_set = sem("s_set")
        s_link = sem("s_link")
        s_turned = sem("s_turned")
        s_table = sem("s_table")
        s_cols = sem("s_cols")
        s_b2 = sem("s_b2")
        s_acc0 = sem("s_acc0")
        s_wsplit = sem("s_wsplit")
        s_wlow = sem("s_wlow")
        e_landed = [sem(f"e_landed{s}") for s in range(ERING)]
        g_landed = [sem(f"g_landed{s}") for s in range(ERING)]
        idx_copied = sem("idx_copied")
        m_hi_done = sem("m_hi_done")
        rel_done = sem("rel_done")
        m_done = sem("m_done")
        m_used = sem("m_used")
        x_landed = sem("x_landed")
        h_done = sem("h_done")
        h_turned = sem("h_turned")
        hT_hi_done = sem("hT_hi_done")
        hT_done = sem("hT_done")
        z_ready = sem("z_ready")
        z_read = sem("z_read")
        z_done = sem("z_done")
        o_ready = sem("o_ready")
        sums_done = sem("sums_done")
        h2_done = sem("h2_done")
        sq_done = sem("sq_done")
        acc1_done = sem("acc1_done")
        acc_done = sem("acc_done")
        spilled = sem("spilled")
        s_gb = sem("s_gb")
        s_tot = sem("s_tot")
        s_bn = sem("s_bn")
        s_bn_act = sem("s_bn_act")
        xt_landed = [sem(f"xt_landed{s}") for s in range(2)]
        back_landed = [sem(f"back_landed{s}") for s in range(2)]
        out_landed = [sem(f"out_landed{s}") for s in range(2)]
        pre_ready = sem("pre_ready")
        scaled = sem("scaled")
        u_done = sem("u_done")
        u_self = sem("u_self")
        stat_self = sem("stat_self")
        var_done = sem("var_done")
        std_done = sem("std_done")
        rstd_done = sem("rstd_done")
        shift_done = sem("shift_done")
        norm_done = sem("norm_done")

        block = ctx.enter_context(nc.Block())

        def by_parity(eng, g, do):
            with eng.If(g % 2 == 0):
                do(0)
            with eng.Else():
                do(1)

        def look_up(eng, n, row, low, high):
            return eng.value_load(table[0:1, row, bass.ds(n, 1)], min_val=low, max_val=high)

        MOST = CH_A
        MOST_ROUNDS = -(-MOST // STEPS_PER_TILE) * TP

        def first_row(eng, n): return look_up(eng, n, 0, 0, E)
        def first_col(eng, n): return look_up(eng, n, 1, 0, CH_A + CH_B - 1)
        def chunks(eng, n): return look_up(eng, n, 2, 1, MOST)
        def rounds_before(eng, p): return look_up(eng, p, 3, 0, MOST_ROUNDS)
        def rounds(eng, p, pairs=1): return rounds_before(eng, p), rounds_before(eng, p + pairs)

        def rows_of(array, pair):
            return rows_from(array, pair * PAIR)

        def rows_from(array, start):
            rows = array[start:start + PAIR, :] if isinstance(start, int) else array[bass.ds(start, PAIR), :]
            return rows.rearrange("(a p) d -> p a d", p=P)

        def pick(buf, slot, rows=P):
            if isinstance(slot, int):
                return buf[0:rows, slot]
            view = buf[0:rows, bass.ds(slot, 1)]
            rest = " ".join("abc"[:len(view.shape) - 2])
            return view.rearrange(f"p o {rest} -> p (o {rest[0]}) {rest[1:]}")

        @block.sync
        def _(sp):
            sp.wait_ge(s_fill, 1)
            sp.dma_start(dst_a[0:CH_A - 1, :], dst[0:(CH_A - 1) * P].rearrange("(c p) -> c p", p=P)).then_inc(s_idx, 16)
            sp.dma_start(dst_a[CH_A - 1:CH_A, P - TAIL_A:P], dst[E - TAIL_A:E].rearrange("(c p) -> c p", c=1)).then_inc(s_idx, 16)
            sp.dma_start(dst_b[0:CH_B - 1, :], dst[GRAN:GRAN + (CH_B - 1) * P].rearrange("(c p) -> c p", p=P)).then_inc(s_idx, 16)
            sp.dma_start(dst_b[CH_B - 1:CH_B, P - TAIL_B:P], dst[E - TAIL_B:E].rearrange("(c p) -> c p", c=1)).then_inc(s_idx, 16)
            sp.dma_start(src_a[0:CH_A - 1, :], src[0:(CH_A - 1) * P].rearrange("(c p) -> c p", p=P)).then_inc(s_idx, 16)
            sp.dma_start(src_a[CH_A - 1:CH_A, :], src[LAST_ROW:E].rearrange("(c p) -> c p", c=1)).then_inc(s_idx, 16)
            sp.dma_start(src_b[0:CH_B - 1, :], src[GRAN:GRAN + (CH_B - 1) * P].rearrange("(c p) -> c p", p=P)).then_inc(s_idx, 16)
            sp.dma_start(src_b[CH_B - 1:CH_B, :], src[LAST_ROW:E].rearrange("(c p) -> c p", c=1)).then_inc(s_idx, 16)
            sp.dma_start(w_raw[:, 0], w1.rearrange("(k p) d -> p k d", p=P)).then_inc(s_w, 16)
            sp.dma_start(w_raw[:, 1], w2.rearrange("(k p) d -> p k d", p=P)).then_inc(s_w, 16)
            sp.wait_ge(s_table, 1)

            def wait_for(held, held_value, semaphore, value):
                sp.wait_ge(held, held_value)
                sp.wait_ge(semaphore, value)

            def load_edges(p):
                rows0 = [first_row(sp, 2 * p + a) for a in range(2)]
                g0, g1 = rounds(sp, p)
                with sp.Fori(g0, g1) as g:
                    rows, free = [], []
                    for t in range(ROUND):
                        row = rows0[t // STEPS_PER_TILE] + ((g - g0) * STEPS_PER_TILE + t % STEPS_PER_TILE) * P
                        over = row > LAST_ROW
                        rows.append(sp.snap((row - over * (row - LAST_ROW)).with_bounds(min_val=0, max_val=LAST_ROW)))
                        free.append(sp.snap(g * ROUND + t + 1))

                    def load(par):
                        for t in range(ROUND):
                            s = par * ROUND + t
                            wait_for(s_table, 1, m_done, free[t])
                            sp.dma_start(mess[:, s, :], edge[bass.ds(rows[t], P), :]).then_inc(e_landed[s], 16)
                    by_parity(sp, g, load)

            with sp.Fori(0, PAIRS + 1) as p:
                load_edges(p)

            for par in range(2):
                sp.wait_ge(norm_done, par + 1)
                sp.dma_start(rows_of(out, par + KEPT), u_out[:, par, :, :]).then_inc(out_landed[par], 16)
                sp.wait_ge(u_done, par + 3)
                sp.dma_start(store[:, 2 * par:2 * par + 2, :], rows_of(h2_dram, par)).then_inc(back_landed[par], 16)
            with sp.Fori(1, SPILLED // 2) as j:
                for par in range(2):
                    q = j * 2 + par
                    start, before = sp.snap((q + KEPT) * PAIR), sp.snap(j * 16)
                    wait_for(s_bn, 8, out_landed[par], before)
                    wait_for(s_bn, 8, norm_done, q + 1)
                    sp.dma_start(rows_from(out, start), pick(u_out, q % TRING)).then_inc(out_landed[par], 16)
                    start = sp.snap(q * PAIR)
                    wait_for(s_bn, 8, u_done, q + 3)
                    wait_for(s_bn, 8, back_landed[par], before)
                    sp.dma_start(store[:, bass.ds(2 * q, 2), :], rows_from(h2_dram, start)).then_inc(back_landed[par], 16)

            def finish(lo, hi, shift_rows):
                with sp.Fori(lo, hi) as j:
                    for par in range(2):
                        q = j * 2 + par
                        start, before = sp.snap((q - shift_rows) * PAIR), sp.snap(j * 16)
                        wait_for(s_bn, 8, out_landed[par], before)
                        wait_for(s_bn, 8, norm_done, q + 1)
                        sp.dma_start(rows_from(out, start), pick(u_out, q % TRING)).then_inc(out_landed[par], 16)
            finish(SPILLED // 2, KEPT // 2, 0)
            finish(KEPT // 2, LOOPED // 2, KEPT)
            sp.wait_ge(norm_done, LOOPED + 1)
            sp.wait_ge(out_landed[0], 16 * (LOOPED // 2))
            sp.dma_start(rows_of(out, PAIRS - 1), u_out[:, LOOPED % TRING, :, :]).then_inc(out_landed[0], 16)
            sp.wait_ge(norm_done, LOOPED + 2)
            sp.wait_ge(out_landed[1], 16 * (LOOPED // 2))
            sp.dma_start(out[N - REST:N, :], u_out[0:REST, (LOOPED + 1) % TRING, 0, :]).then_inc(out_landed[1], 16)
            for par in range(2):
                sp.wait_ge(out_landed[par], 16 * (LOOPED // 2 + 1))

        @block.gpsimd
        def _(pool):
            nc.gpsimd.memset(dst_a, -1)
            nc.gpsimd.memset(dst_b, -1).then_inc(s_fill, 1)
            nc.gpsimd.memset(ones[:], 1.0).then_inc(s_const, 1)
            pool.wait_ge(s_const, 1)
            nc.gpsimd.affine_select(out=ident[:], in_=ones[:], compare_op=ALU.is_equal, fill=0.0, base=0,
                                    pattern=[[1, P]], channel_multiplier=-1)
            nc.gpsimd.affine_select(out=upper, in_=ones[0:TP, 0:TPR], compare_op=ALU.is_gt, fill=0.0, base=0,
                                    pattern=[[1, TPR]], channel_multiplier=-1)
            nc.gpsimd.iota(iota_row[:], pattern=[[1, P]], base=0, channel_multiplier=0,
                           allow_small_or_imprecise_dtypes=True)
            nc.gpsimd.iota(iota_n, pattern=[[1, TN]], base=0, channel_multiplier=0,
                           allow_small_or_imprecise_dtypes=True)
            nc.gpsimd.iota(tile_off[:], pattern=[[P, TN]], base=0, channel_multiplier=0,
                           allow_small_or_imprecise_dtypes=True)
            nc.gpsimd.iota(gran, pattern=[[1, 2]], base=0, channel_multiplier=2,
                           allow_small_or_imprecise_dtypes=True).then_inc(s_const, 1)
            nc.gpsimd.memset(acc1[:], 0.0)
            nc.gpsimd.memset(acc2[:], 0.0).then_inc(s_acc0, 1)
            pool.wait_ge(s_acc0, 1)

            def gathers(p):
                tiles = [2 * p, 2 * p + 1]
                cols0 = [first_col(pool, n) for n in tiles]
                counts = [chunks(pool, n) for n in tiles]
                g0, g1 = rounds(pool, p)
                with pool.Fori(g0, g1) as g:
                    def gather(par):
                        for t in range(ROUND):
                            a = t // STEPS_PER_TILE
                            s = par * ROUND + t
                            nth = (g - g0) * STEPS_PER_TILE + t % STEPS_PER_TILE
                            beyond = nth - counts[a] > -1
                            col = cols0[a] + nth
                            col = (col + beyond * (NOTHING - col)).with_bounds(min_val=0, max_val=NOTHING)
                            step = g * ROUND + t
                            pool.wait_ge(m_done, step + 1)
                            pool.wait_ge(e_landed[s], (g // 2) * 16 + 16)
                            nc.gpsimd.tensor_copy(idx[s][:], src_col[:, bass.ds(col, 1)]).then_inc(idx_copied, 1)
                            nc.gpsimd.tensor_tensor(rel[:, s:s + 1], dst_col[:, bass.ds(col, 1)], tile_off[:, bass.ds(tiles[a], 1)], ALU.subtract).then_inc(rel_done, 1)
                            pool.wait_ge(s_cols, 1)
                            pool.wait_ge(idx_copied, step + 1)
                            nc.gpsimd.indirect_dma_start(
                                out=mess[:, s, :], out_offset=None, in_=x,
                                in_offset=bass.IndirectOffsetOnAxis(ap=idx[s][:, 0:1], axis=0),
                                compute_op=ALU.add,
                            ).then_inc(g_landed[s], 16)
                    by_parity(pool, g, gather)

            def add_up(n, a, slot, rows):
                pool.wait_ge(sq_done, n + 1)
                pool.wait_ge(acc_done, n + 2)
                nc.gpsimd.tensor_tensor(acc2[0:rows, :], acc2[0:rows, :], sq[0:rows, a, :], ALU.add).then_inc(acc_done, 1)

            pool.sem_inc(acc_done, 2)
            pool.wait_ge(s_table, 1)
            pool.wait_ge(s_cols, 1)
            with pool.Fori(0, 3) as p:
                gathers(p)

            def body(i, slot_before):
                if slot_before is not None:
                    for a in range(2):
                        add_up(2 * i - 2 + a, a, slot_before + a, P)
                gathers(i + 3)
            body(0, None)
            with pool.Fori(1, KEPT + 1) as i:
                body(i, 2 * i - 2)
            with pool.Fori(KEPT + 1, PAIRS - 3) as i:
                body(i, 2 * i - 2 - 2 * KEPT)
            for i in range(PAIRS - 3, PAIRS):
                for a in range(2):
                    add_up(2 * i - 2 + a, a, 2 * i - 2 - 2 * KEPT + a, P)
                if i == PAIRS - 3:
                    gathers(PAIRS)
            for a in range(2):
                add_up(2 * PAIRS - 2 + a, a, 2 * KEPT + a, P)
            add_up(TILES - 1, 0, 2 * KEPT + 2, REST)

            pool.wait_ge(s_bn, 6)

            def scale(slot):
                for a in range(2):
                    s = slot + a
                    h2 = pick(store, s)
                    last = nc.gpsimd.tensor_tensor(h2, h2, bn_a[:], ALU.mult)
                last.then_inc(scaled, 1)
            with pool.Fori(0, KEPT) as q:
                scale(2 * q)
            with pool.Fori(0, SPILLED // 2) as j:
                for par in range(2):
                    pool.wait_ge(back_landed[par], j * 16 + 16)
                    scale(4 * j + 2 * par)
            scale(2 * KEPT)
            h2 = store[0:REST, 2 * KEPT + 2, :]
            nc.gpsimd.tensor_tensor(h2, h2, bn_a[0:REST, :], ALU.mult).then_inc(scaled, 1)

        @block.scalar
        def _(act):
            act.dma_start(b1_col[:], b1.rearrange("(k p) -> p k", p=P), allow_slow_non_contiguous=True).then_inc(s_bias, 16)
            act.dma_start(b2_all, b2.rearrange("(o d) -> o d", o=1).broadcast_to([64, D])).then_inc(s_bias, 16)
            act.sem_inc(z_read, 2)
            act.wait_ge(s_w, 32)
            for w in range(2):
                nc.scalar.copy(w_hi[w][:], w_raw[:, w]).then_inc(s_wsplit, 1)

            act.dma_start(x_in[:, 0, :, :], rows_of(x, 0)).then_inc(x_landed, 16)
            act.wait_ge(x_landed, 16)
            act.dma_start(x_in[:, 1, :, :], rows_of(x, 1)).then_inc(x_landed, 16)

            def hT_high(n, a, rows):
                act.wait_ge(h_turned, n + 3)
                nc.scalar.copy(hT_hi[:, :, a * P:a * P + rows], ps_turn[a][:, :, 0:rows]).then_inc(hT_hi_done, 1)

            def m_high(g_range):
                with act.Fori(g_range[0], g_range[1]) as g:
                    def high(par):
                        for t in range(ROUND):
                            s = par * ROUND + t
                            act.wait_ge(g_landed[s], (g // 2) * 16 + 16)
                            act.wait_ge(m_used, g * ROUND + t + 1)
                            nc.scalar.activation(m_hi[:, t, :], mess[:, s, :], ACT.Relu).then_inc(m_hi_done, 1)
                    by_parity(act, g, high)

            act.wait_ge(s_table, 1)
            m_high(rounds(act, 0, 2))
            act.wait_ge(s_bias, 32)
            for a in range(2):
                hT_high(a, a, P)

            def z_high(i, cols, blocks=range(KB)):
                for f in blocks:
                    act.wait_ge(z_ready, 4 * i + f + 1)
                    act.wait_ge(z_done, 4 * i + f + 1)
                    nc.scalar.activation(z_full[:, f % 2, 0:cols], ps_z[f % 2][:, 0:cols], ACT.Relu, bias=b1_col[:, f:f + 1])
                    nc.scalar.activation(zT_hi[:, f, 0:cols], ps_z[f % 2][:, 0:cols], ACT.Relu, bias=b1_col[:, f:f + 1]).then_inc(z_read, 1)

            def squares(n, a, slot, rows):
                act.wait_ge(h2_done, n + 3)
                act.wait_ge(acc_done, n + 1)
                h2 = pick(store, slot, rows)
                nc.scalar.activation(sq[0:rows, a, :], h2, ACT.Square).then_inc(sq_done, 1)

            def body(i, slot, spill):
                z_high(i, PAIR, (0, 1))
                next_rounds = rounds(act, i + 2)
                z_high(i, PAIR, (2, 3))
                m_high(next_rounds)
                for a in range(2):
                    hT_high(2 * i + 2 + a, a, P)
                for a in range(2):
                    squares(2 * i + a, a, slot + a, P)
                act.dma_start(pick(x_in, i % 2), rows_of(x, i + 2)).then_inc(x_landed, 16)
                if spill:
                    act.dma_start(rows_of(h2_dram, i), store[:, bass.ds(slot, 2), :]).then_inc(spilled, 16)
            with act.Fori(0, SPILLED) as i:
                body(i, 2 * i, True)
            with act.Fori(SPILLED, KEPT) as i:
                body(i, 2 * i, False)
            with act.Fori(KEPT, LOOPED - 1) as i:
                body(i, 2 * i - 2 * KEPT, False)
            i = LOOPED - 1
            z_high(i, PAIR)
            m_high(rounds(act, PAIRS))
            for a in range(2):
                hT_high(2 * i + 2 + a, a, P)
            for a in range(2):
                squares(2 * i + a, a, 2 * i - 2 * KEPT + a, P)
            act.dma_start(x_in[0:REST, PAIRS % 2, 0, :], x[N - REST:N, :]).then_inc(x_landed, 16)
            i = PAIRS - 1
            z_high(i, PAIR)
            hT_high(2 * i + 2, 0, REST)
            for a in range(2):
                squares(2 * i + a, a, 2 * KEPT + a, P)
            z_high(PAIRS, REST)
            squares(TILES - 1, 0, 2 * KEPT + 2, REST)

            def load_tail(q, pair, par):
                act.dma_start(pick(x_tail, q % TRING), rows_of(x, pair)).then_inc(xt_landed[par], 16)

            act.wait_ge(acc_done, TILES + 2)
            act.wait_ge(o_ready, TILES)
            act.dma_start(gamma_all[:], gamma.rearrange("(o d) -> o d", o=1).broadcast_to([P, D])).then_inc(s_gb, 16)
            act.dma_start(beta_all[:], beta.rearrange("(o d) -> o d", o=1).broadcast_to([P, D])).then_inc(s_gb, 16)
            load_tail(0, KEPT, 0)
            load_tail(1, KEPT + 1, 1)
            act.wait_ge(s_tot, 1)
            nc.scalar.mul(bn_mean[:], ps_z[0][:], 1.0 / N).then_inc(s_bn_act, 1)
            act.wait_ge(s_tot, 2)
            nc.scalar.mul(bn_sq[:], ps_z[1][:], 1.0 / N).then_inc(s_bn_act, 1)
            act.wait_ge(s_bn, 2)
            nc.scalar.activation(bn_std[:], bn_var[:], ACT.Sqrt, bias=eps_bn[:]).then_inc(s_bn_act, 1)

            def root(q, slot, par, rows, tiles):
                act.wait_ge(var_done, q + 1)
                nc.scalar.activation(pick(std, slot, rows)[:, 0:tiles], mean_var[0:rows, par, 0:tiles, 1], ACT.Sqrt, bias=eps_ln[0:rows, :]).then_inc(std_done, 1)

            def norm(q, slot, rows, tiles):
                act.wait_ge(shift_done, q + 1)
                for a in range(tiles):
                    u = pick(u_out, slot, rows)[:, a, :]
                    last = nc.scalar.activation(u, u, ACT.Identity, bias=pick(shift, slot, rows)[:, a:a + 1], scale=pick(rstd, slot, rows)[:, a:a + 1])
                last.then_inc(norm_done, 1)

            def tail_body(q, j, par, pair_ahead):
                if pair_ahead is not None:
                    act.wait_ge(pre_ready, q + 1)
                    act.wait_ge(xt_landed[par], j * 16 + 16)
                    load_tail(q + 2, pair_ahead, par)
                root(q, q % TRING, par, P, 2)
                norm(q - 1, (q + TRING - 1) % TRING, P, 2)

            act.wait_ge(xt_landed[0], 16)
            load_tail(2, KEPT + 2, 0)
            root(0, 0, 0, P, 2)
            act.wait_ge(xt_landed[1], 16)
            load_tail(3, KEPT + 3, 1)
            root(1, 1, 1, P, 2)
            norm(0, 0, P, 2)
            for lo, hi, pair_shift in ((1, SPILLED // 2 - 1, KEPT), (SPILLED // 2 - 1, KEPT // 2 - 1, 0),
                                       (KEPT // 2 - 1, LOOPED // 2 - 1, -KEPT)):
                with act.Fori(lo, hi) as j:
                    for par in range(2):
                        q = 2 * j + par
                        tail_body(q, j, par, q + 2 + pair_shift)
            j = LOOPED // 2 - 1
            q = 2 * j
            act.wait_ge(pre_ready, q + 1)
            act.wait_ge(xt_landed[0], 16 * (j + 1))
            load_tail(q + 2, PAIRS - 1, 0)
            root(q, q % TRING, 0, P, 2)
            norm(q - 1, (q - 1) % TRING, P, 2)
            act.wait_ge(pre_ready, q + 2)
            act.wait_ge(xt_landed[1], 16 * (j + 1))
            act.dma_start(x_tail[0:REST, (q + 3) % TRING, 0, :], x[N - REST:N, :]).then_inc(xt_landed[1], 16)
            root(q + 1, (q + 1) % TRING, 1, P, 2)
            norm(q, q % TRING, P, 2)
            root(LOOPED, LOOPED % TRING, 0, P, 2)
            norm(LOOPED - 1, (LOOPED - 1) % TRING, P, 2)
            root(LOOPED + 1, (LOOPED + 1) % TRING, 1, REST, 1)
            norm(LOOPED, LOOPED % TRING, P, 2)
            norm(LOOPED + 1, (LOOPED + 1) % TRING, REST, 1)

        @block.tensor
        def _(pe):
            mm = nc.tensor.matmul
            pe.sem_inc(m_used, ROUND)
            pe.sem_inc(h_turned, 2)
            pe.sem_inc(pre_ready, 2)
            pe.wait_ge(s_const, 2)
            pe.wait_ge(s_set, 1)
            cols = ps_turn[0][:, :, :]
            nc.tensor.transpose(ps_turn[0][:, 0, 0:CH_A], dst_af, ident[0:CH_A, 0:CH_A])
            nc.tensor.transpose(ps_turn[0][:, 1, 0:CH_B], dst_bf, ident[0:CH_B, 0:CH_B])
            nc.tensor.transpose(ps_turn[0][:, 2, 0:CH_A], src_af, ident[0:CH_A, 0:CH_A])
            nc.tensor.transpose(ps_turn[0][:, 3, 0:CH_B], src_bf, ident[0:CH_B, 0:CH_B]).then_inc(s_turned, 1)
            pe.wait_ge(s_set, 2)
            nc.tensor.transpose(ps_turn[1][0:TN, 0, 0:CH_A], range_f, ident[0:CH_A, 0:CH_A])
            nc.tensor.transpose(ps_turn[1][0:TN, 1, 0:CH_A], range_l, ident[0:CH_A, 0:CH_A]).then_inc(s_turned, 1)
            pe.wait_ge(s_set, 3)
            mm(ps_z[0][0:1, 0:TN], nf[:, 8:9], ident[0:TN, 0:TN], start=True, stop=True)
            mm(ps_z[0][0:1, TN:2 * TN], nf[:, 9:10], ident[0:TN, 0:TN], start=True, stop=True)
            mm(ps_z[0][0:1, 2 * TN:3 * TN], nf[:, 10:11], ident[0:TN, 0:TN], start=True, stop=True).then_inc(s_turned, 1)
            pe.wait_ge(s_set, 4)
            mm(ps_z[1][0:TP, 0:1], rounds_f, ones[0:1, 0:1], start=True, stop=True).then_inc(s_turned, 1)
            pe.wait_ge(s_set, 5)
            mm(ps_z[1][0:1, 0:TPR], rounds_col, upper, start=True, stop=True).then_inc(s_turned, 1)
            pe.wait_ge(s_table, 1)

            def pair_sums(p):
                g0, g1 = rounds(pe, p)
                pe.wait_ge(h_done, 2 * p + 2)

                def one(g, first):
                    for t in range(ROUND):
                        a = t // STEPS_PER_TILE
                        pe.wait_ge(m_done, g * ROUND + t + ERING + 1)
                        mm(ps_sum[a][:], onehot[:, t, :], m_hi[:, t, :], start=first and t % STEPS_PER_TILE == 0, stop=False, skip_group_check=True)
                        mm(ps_sum[a][:], onehot[:, t, :], m_lo[:, t, :], start=False, stop=True,
                           skip_group_check=True).then_inc(m_used, 1)
                one(g0, True)
                with pe.If(g1 > g0 + 1):
                    with pe.Fori(g0 + 1, g1) as g:
                        one(g, False)
                with pe.Else():
                    pe.nop()

            def turn(n, a, rows):
                pe.wait_ge(h_done, n + 3)
                pe.wait_ge(hT_done, n + 1)
                for k in range(KB):
                    t = nc.tensor.transpose(ps_turn[a][:, k, 0:rows], h[0:rows, a, k * P:(k + 1) * P], ident[0:rows, 0:rows])
                t.then_inc(h_turned, 1)

            def layer1(i, cols, tiles_done):
                pe.wait_ge(hT_hi_done, tiles_done)
                for f in range(KB):
                    pe.wait_ge(z_read, 4 * i + f + 1)
                    out_ = ps_z[f % 2][:, 0:cols]
                    parts = [(w_hi[0], hT_hi), (w_lo[0], hT_hi), (w_hi[0], hT_lo)]
                    for m in range(3 * KB):
                        w, r = parts[m // KB]
                        if f == 0 and m == 2 * KB:
                            pe.wait_ge(hT_done, tiles_done + 2)
                        t = mm(out_, w[:, m % KB, f * P:(f + 1) * P], r[:, m % KB, 0:cols], start=(m == 0), stop=(m == 3 * KB - 1))
                        if f == 0 and m == 0:
                            t.then_inc(sums_done, 1)
                    t.then_inc(z_ready, 1)

            def layer2(i, n, a):
                pe.wait_ge(h2_done, n + 1)
                mm(ps_o[a][:], row_pick[:], row_parts[:], start=True, stop=False)
                for f in range(KB):
                    pe.wait_ge(z_done, 4 * i + f + 3)
                    for m, (l, w) in enumerate(((zT_hi, w_hi[1]), (zT_hi, w_lo[1]), (zT_lo, w_hi[1]))):
                        t = mm(ps_o[a][:], l[:, f, a * P:(a + 1) * P], w[:, f, :], start=False, stop=(f == KB - 1 and m == 2))
                t.then_inc(o_ready, 1)

            pe.wait_ge(s_wlow, 2)
            pe.wait_ge(s_b2, 4)
            pair_sums(0)
            for a in range(2):
                turn(a, a, P)
            with pe.Fori(0, LOOPED) as i:
                pair_sums(i + 1)
                layer1(i, PAIR, 2 * i + 2)
                layer2(i, 2 * i, 0)
                for a in range(2):
                    turn(2 * i + 2 + a, a, P)
                layer2(i, 2 * i + 1, 1)
            i = PAIRS - 1
            pair_sums(PAIRS)
            layer1(i, PAIR, 2 * i + 2)
            layer2(i, 2 * i, 0)
            turn(TILES - 1, 0, REST)
            layer2(i, 2 * i + 1, 1)
            layer1(PAIRS, REST, TILES)
            layer2(PAIRS, TILES - 1, 0)

            pe.wait_ge(acc_done, TILES + 2)
            pe.wait_ge(acc1_done, TILES + 1)
            mm(ps_z[0][:], ones[:], acc1[:], start=True, stop=True).then_inc(s_tot, 1)
            mm(ps_z[1][:], ones[:], acc2[:], start=True, stop=True).then_inc(s_tot, 1)

            def pre(q, slot, par, rows, tiles):
                pe.wait_ge(u_done, q + 1)
                for a in range(tiles):
                    bank = tail_banks[par][a]
                    mm(bank[:], row_pick[:], row_parts[:], start=True, stop=False, skip_group_check=True)
                    t = mm(bank[0:rows, :] if rows == P else bank[:], ident[:] if rows == P else ident[0:rows, :],
                           pick(x_tail, slot, rows)[:, a, :], start=False, stop=True, skip_group_check=True)
                t.then_inc(pre_ready, 1)
            pe.wait_ge(s_bn, 8)
            with pe.Fori(0, LOOPED // 2) as j:
                for par in range(2):
                    q = j * 2 + par
                    pe.wait_ge(xt_landed[par], j * 16 + 16)
                    pre(q, q % TRING, par, P, 2)
            pe.wait_ge(xt_landed[0], 16 * (LOOPED // 2 + 1))
            pre(LOOPED, LOOPED % TRING, 0, P, 2)
            pe.wait_ge(xt_landed[1], 16 * (LOOPED // 2 + 1))
            pre(LOOPED + 1, (LOOPED + 1) % TRING, 1, REST, 1)

        @block.vector
        def _(dve):
            v = nc.vector
            dve.sem_inc(m_done, ERING)
            dve.sem_inc(acc1_done, 1)
            dve.sem_inc(h_done, 2)
            dve.sem_inc(hT_done, 2)
            dve.sem_inc(z_done, 2)
            dve.sem_inc(h2_done, 2)
            dve.sem_inc(u_done, 2)
            chain = [0]
            def link(ins):
                chain[0] += 1
                ins.then_inc(s_link, 1)
                dve.wait_ge(s_link, chain[0])

            dve.wait_ge(s_idx, 16 * 8)
            v.tensor_copy(dst_af, dst_a)
            v.tensor_copy(dst_bf, dst_b)
            v.tensor_copy(src_af, src_a)
            v.tensor_copy(src_bf, src_b).then_inc(s_set, 1)
            link(v.tensor_scalar(tile_i, dst_a, 7, None, ALU.arith_shift_right))
            link(v.tensor_copy(tile_f, tile_i))
            link(v.tensor_scalar(tile_up, tile_f, 0.0, float(FAR), ALU.is_lt, ALU.mult))
            link(v.tensor_tensor(tile_up, tile_up, tile_f, ALU.add))
            v.tensor_reduce(t_max, tile_f.rearrange("c (g e) -> c g e", g=2), AX_X, ALU.max)
            link(v.tensor_reduce(t_min, tile_up.rearrange("c (g e) -> c g e", g=2), AX_X, ALU.min))
            dve.wait_ge(s_const, 2)
            link(v.tensor_scalar(gran_up, gran, float(LAST_GRAN), None, ALU.min))
            v.tensor_scalar(gran_last, gran_up, 1.0, None, ALU.add)
            link(v.tensor_scalar(gran_first, gran_up, -1.0, float(FAR), ALU.mult, ALU.add))
            for g in range(2):
                v.tensor_scalar(above[0:CH_A, :] if g == 0 else cover[1], iota_n[0:CH_A, :], t_min[:, g:g + 1], None, ALU.is_ge)
            link(v.tensor_scalar(part_f[0], iota_n[0:CH_A, :], t_max[:, 0:1], None, ALU.is_le))
            link(v.tensor_scalar(part_f[1], iota_n[0:CH_A, :], t_max[:, 1:2], None, ALU.is_le))
            link(v.tensor_tensor(cover[0], above[0:CH_A, :], part_f[0], ALU.mult))
            link(v.tensor_tensor(cover[1], cover[1], part_f[1], ALU.mult))
            for g in range(2):
                v.tensor_scalar(part_f[g], cover[g], gran_first[:, g:g + 1], None, ALU.mult)
                link(v.tensor_scalar(part_l[g], cover[g], gran_last[:, g:g + 1], None, ALU.mult))
            v.tensor_tensor(range_f, part_f[0], part_f[1], ALU.max)
            v.tensor_tensor(range_l, part_l[0], part_l[1], ALU.max).then_inc(s_set, 1)
            dve.wait_ge(s_turned, 1)
            v.memset(dst_col[:, NOTHING:NOTHING + 1], -1.0)
            v.memset(src_col[:, NOTHING:NOTHING + 1], 0)
            v.tensor_copy(dst_col[:, 0:CH_A], ps_turn[0][:, 0, 0:CH_A])
            v.tensor_copy(dst_col[:, CH_A:CH_A + CH_B], ps_turn[0][:, 1, 0:CH_B])
            v.tensor_copy(src_col[:, 0:CH_A], ps_turn[0][:, 2, 0:CH_A])
            v.tensor_copy(src_col[:, CH_A:CH_A + CH_B], ps_turn[0][:, 3, 0:CH_B]).then_inc(s_cols, 1)
            dve.wait_ge(s_turned, 2)
            v.tensor_reduce(nf[:, 0:1], ps_turn[1][0:TN, 0, 0:CH_A], AX_X, ALU.max)
            link(v.tensor_reduce(nf[:, 1:2], ps_turn[1][0:TN, 1, 0:CH_A], AX_X, ALU.max))
            v.tensor_scalar(nf[:, 2:3], nf[:, 1:2], 1.0, None, ALU.is_ge)
            v.tensor_scalar(nf[:, 3:4], nf[:, 0:1], -1.0, float(FAR), ALU.mult, ALU.add)
            link(v.tensor_scalar(nf[:, 4:5], nf[:, 1:2], -1.0, 0.0, ALU.add, ALU.max))
            link(v.tensor_tensor(nf[:, 5:6], nf[:, 3:4], nf[:, 2:3], ALU.mult))
            link(v.tensor_tensor(nf[:, 6:7], nf[:, 4:5], nf[:, 5:6], ALU.subtract))
            v.tensor_copy(ni[:, 0:1], nf[:, 6:7])
            link(v.tensor_copy(ni[:, 1:2], nf[:, 5:6]))
            v.tensor_scalar(ni[:, 2:4], ni[:, 0:2], 1, None, ALU.arith_shift_right)
            link(v.tensor_scalar(ni[:, 4:5], ni[:, 1:2], 1, None, ALU.bitwise_and))
            link(v.tensor_copy(nf[:, 11:14], ni[:, 2:5]))
            v.tensor_scalar(nf[:, 8:9], nf[:, 5:6], float(GRAN), None, ALU.mult)
            v.tensor_scalar(nf[:, 10:11], nf[:, 11:12], 1.0, None, ALU.add)
            v.scalar_tensor_tensor(nf[:, 9:10], nf[:, 13:14], float(CH_A), nf[:, 12:13], ALU.mult, ALU.add).then_inc(s_set, 1)
            assert STEPS_PER_TILE == 2
            dve.wait_ge(s_turned, 3)
            v.tensor_copy(table[0:1, 0:3, :].rearrange("o r n -> o (r n)"), ps_z[0][0:1, 0:3 * TN])
            link(v.tensor_reduce(most, ps_z[0][0:1, 2 * TN:3 * TN].rearrange("o (p a) -> o p a", a=2), AX_X, ALU.max))
            link(v.tensor_scalar(rounds_up, most, 1.0, None, ALU.add))
            link(v.tensor_copy(rounds_i, rounds_up))
            link(v.tensor_scalar(rounds_half, rounds_i, 1, None, ALU.arith_shift_right))
            v.tensor_copy(rounds_f, rounds_half).then_inc(s_set, 1)
            dve.wait_ge(s_turned, 4)
            v.tensor_copy(rounds_col, ps_z[1][0:TP, 0:1]).then_inc(s_set, 1)
            dve.wait_ge(s_turned, 5)
            v.tensor_copy(table[0:1, 3, 0:TPR], ps_z[1][0:1, 0:TPR]).then_inc(s_table, 1)
            v.memset(row_pick[:].bitcast(F32), 0.0).then_inc(s_b2, 1)
            dve.wait_ge(s_b2, 1)
            v.memset(row_pick[0:1, :].bitcast(F32), 1.0)
            v.memset(row_pick[32:33, :].bitcast(F32), 1.0).then_inc(s_b2, 1)
            dve.wait_ge(s_bias, 32)
            v.tensor_copy(row_parts[:], b2_all).then_inc(s_b2, 1)
            dve.wait_ge(s_b2, 3)
            v.tensor_tensor(row_parts[32:64, :], b2_all[32:64, :], row_parts[32:64, :].bitcast(F32), ALU.subtract).then_inc(s_b2, 1)
            dve.wait_ge(s_b2, 4)
            for w in range(2):
                dve.wait_ge(s_wsplit, w + 1)
                v.tensor_tensor(w_lo[w][:], w_raw[:, w], w_hi[w][:].bitcast(F32), ALU.subtract).then_inc(s_wlow, 1)
            dve.wait_ge(s_wlow, 2)

            def m_parts(g_range):
                with dve.Fori(g_range[0], g_range[1]) as g:
                    for t in range(ROUND):
                        slot = (g % 2) * ROUND + t
                        dve.wait_ge(m_hi_done, g * ROUND + t + 1)
                        v.scalar_tensor_tensor(m_lo[:, t, :], pick(mess, slot), 0.0, m_hi[:, t, :].bitcast(F32), ALU.max, ALU.subtract)
                        dve.wait_ge(rel_done, g * ROUND + t + 1)
                        v.tensor_scalar(onehot[:, t, :], iota_row[:], rel[:, bass.ds(slot, 1)], None, ALU.is_equal).then_inc(m_done, 1)

            def make_h(n, a, i, slot, rows):
                if not (isinstance(i, int) and i == 0):
                    dve.wait_ge(sums_done, i)
                dve.wait_ge(x_landed, 16 * i + 16)
                dve.wait_ge(h_turned, n + 1)
                v.tensor_tensor(h[0:rows, a, :], ps_sum[a][0:rows, :], pick(x_in, slot, rows)[:, a, :], ALU.add).then_inc(h_done, 1)

            def hT_low(n, a, rows):
                dve.wait_ge(hT_hi_done, n + 1)
                v.tensor_tensor(hT_lo[:, :, a * P:a * P + rows], ps_turn[a][:, :, 0:rows],
                                hT_hi[:, :, a * P:a * P + rows].bitcast(F32), ALU.subtract).then_inc(hT_done, 1)

            def z_low(i, f, cols):
                dve.wait_ge(z_read, 4 * i + f + 3)
                v.tensor_tensor(zT_lo[:, f, 0:cols], z_full[:, f % 2, 0:cols], zT_hi[:, f, 0:cols].bitcast(F32), ALU.subtract).then_inc(z_done, 1)

            def make_h2(n, a, i, slot, xslot, rows):
                dve.wait_ge(o_ready, n + 1)
                h2 = pick(store, slot, rows)
                v.tensor_tensor(h2, ps_o[a][0:rows, :], pick(x_in, xslot, rows)[:, a, :], ALU.add).then_inc(h2_done, 1)

            def add_up(n, slot, rows):
                dve.wait_ge(h2_done, n + 3)
                dve.wait_ge(acc1_done, n + 1)
                v.tensor_tensor(acc1[0:rows, :], acc1[0:rows, :], pick(store, slot, rows), ALU.add).then_inc(acc1_done, 1)

            m_parts(rounds(dve, 0))
            dve.wait_ge(m_used, rounds_before(dve, 1) * ROUND + ROUND)
            for a in range(2):
                make_h(a, a, 0, 0, P)
            m_parts(rounds(dve, 1))
            for a in range(2):
                hT_low(a, a, P)

            def body(i, slot):
                for f in range(2):
                    z_low(i, f, PAIR)
                next_rounds = rounds(dve, i + 2)
                for a in range(2):
                    make_h(2 * i + 2 + a, a, i + 1, (i + 1) % 2, P)
                for f in range(2, KB):
                    z_low(i, f, PAIR)
                m_parts(next_rounds)
                make_h2(2 * i, 0, i, slot, i % 2, P)
                for a in range(2):
                    hT_low(2 * i + 2 + a, a, P)
                make_h2(2 * i + 1, 1, i, slot + 1, i % 2, P)
                for a in range(2):
                    add_up(2 * i + a, slot + a, P)
            with dve.Fori(0, KEPT) as i:
                body(i, 2 * i)
            dve.wait_ge(spilled, 16 * SPILLED)
            with dve.Fori(KEPT, LOOPED) as i:
                body(i, 2 * i - 2 * KEPT)
            i = PAIRS - 1
            make_h(TILES - 1, 0, PAIRS, PAIRS % 2, REST)
            for f in range(KB):
                z_low(i, f, PAIR)
            make_h2(2 * i, 0, i, 2 * KEPT, i % 2, P)
            hT_low(TILES - 1, 0, REST)
            make_h2(2 * i + 1, 1, i, 2 * KEPT + 1, i % 2, P)
            for a in range(2):
                add_up(2 * i + a, 2 * KEPT + a, P)
            for f in range(KB):
                z_low(PAIRS, f, REST)
            make_h2(TILES - 1, 0, PAIRS, 2 * KEPT + 2, PAIRS % 2, REST)
            add_up(TILES - 1, 2 * KEPT + 2, REST)

            dve.wait_ge(o_ready, TILES)
            dve.wait_ge(acc_done, TILES + 2)
            v.memset(eps_bn[:], BN_EPS)
            v.memset(eps_ln[:], LN_EPS)
            dve.wait_ge(s_bn_act, 2)
            v.tensor_tensor(bn_var[:], bn_mean[:], bn_mean[:], ALU.mult).then_inc(s_bn, 1)
            dve.wait_ge(s_bn, 1)
            v.tensor_tensor(bn_var[:], bn_sq[:], bn_var[:], ALU.subtract).then_inc(s_bn, 1)
            dve.wait_ge(s_bn_act, 3)
            v.reciprocal(bn_rstd[:], bn_std[:]).then_inc(s_bn, 1)
            dve.wait_ge(s_bn, 3)
            dve.wait_ge(s_gb, 32)
            v.tensor_tensor(bn_a[:], bn_rstd[:], gamma_all[:], ALU.mult).then_inc(s_bn, 1)
            dve.wait_ge(s_bn, 4)
            v.tensor_tensor(bn_ma[:], bn_mean[:], bn_a[:], ALU.mult).then_inc(s_bn, 1)
            dve.wait_ge(s_bn, 5)
            v.tensor_tensor(bn_c[:], beta_all[:], bn_ma[:], ALU.subtract).then_inc(s_bn, 1)
            dve.wait_ge(s_bn, 6)
            v.tensor_copy(row_parts[0:64, :], bn_c[0:64, :]).then_inc(s_bn, 1)
            dve.wait_ge(s_bn, 7)
            v.tensor_tensor(row_parts[32:64, :], bn_c[32:64, :], row_parts[32:64, :].bitcast(F32), ALU.subtract).then_inc(s_bn, 1)

            def pair_stats(q, slot, par, store_slot, rows, tiles):
                dve.wait_ge(pre_ready, q + 3)
                dve.wait_ge(scaled, q + 1)
                for a in range(tiles):
                    s = store_slot + a
                    t = pick(store, s, rows)
                    last = v.tensor_tensor(pick(u_out, slot, rows)[:, a, :], tail_banks[par][a][0:rows, :], t, ALU.add)
                last.then_inc(u_done, 1)
                dve.wait_ge(s_bn, 8)
                dve.wait_ge(u_done, q + 3)
                for a in range(tiles):
                    st_ = stats[0:rows, par, a, :]
                    last = v.bn_stats(st_, pick(u_out, slot, rows)[:, a, :])
                last.then_inc(stat_self, 1)
                dve.wait_ge(s_bn, 8)
                dve.wait_ge(stat_self, q + 1)
                for a in range(tiles):
                    st_ = stats[0:rows, par, a, :]
                    mv = mean_var[0:rows, par, a, :]
                    last = v.bn_aggr(mv, st_)
                last.then_inc(var_done, 1)

            def scale_shift(q, slot, par, rows, tiles):
                dve.wait_ge(std_done, q + 1)
                v.reciprocal(pick(rstd, slot, rows)[:, 0:tiles], pick(std, slot, rows)[:, 0:tiles]).then_inc(rstd_done, 1)
                dve.wait_ge(rstd_done, q + 1)
                v.scalar_tensor_tensor(pick(shift, slot, rows)[:, 0:tiles], mean_var[0:rows, par, 0:tiles, 0], -1.0,
                                       pick(rstd, slot, rows)[:, 0:tiles], ALU.mult, ALU.mult).then_inc(shift_done, 1)

            pair_stats(0, 0, 0, 0, P, 2)
            pair_stats(1, 1, 1, 2, P, 2)
            scale_shift(0, 0, 0, P, 2)
            for q in (2, 3):
                pair_stats(q, q, q % 2, 2 * q, P, 2)
                scale_shift(q - 1, q - 1, (q - 1) % 2, P, 2)
            for lo, hi, shift_slots in ((2, KEPT // 2, 0), (KEPT // 2, LOOPED // 2, KEPT)):
                with dve.Fori(lo, hi) as j:
                    for par in range(2):
                        q = j * 2 + par
                        dve.wait_ge(out_landed[par], j * 16 - 16)
                        pair_stats(q, q % TRING, par, 2 * q - 2 * shift_slots, P, 2)
                        scale_shift(q - 1, (q + TRING - 1) % TRING, 1 - par, P, 2)
            for q, slot, rows, tiles in ((LOOPED, 2 * KEPT, P, 2), (LOOPED + 1, 2 * KEPT + 2, REST, 1)):
                dve.wait_ge(out_landed[q % 2], 16 * (q // 2 - 1))
                pair_stats(q, q % TRING, q % 2, slot, rows, tiles)
                scale_shift(q - 1, (q - 1) % TRING, (q - 1) % 2, P, 2)
            scale_shift(LOOPED + 1, (LOOPED + 1) % TRING, 1, REST, 1)


_INS = ['x', 'src', 'dst', 'edge_attr_512', 'L0_gnn_W1', 'L0_gnn_b1', 'L0_gnn_W2', 'L0_gnn_b2', 'L0_gnn_gamma', 'L0_gnn_beta']
_OUTS = [((10000, 512), 'float32')]


def kernel(**inputs):
    import numpy as _np
    import concourse.bacc as _bacc
    from concourse import mybir as _mybir
    from concourse.bass_utils import run_bass_kernel_spmd as _run

    nc = _bacc.Bacc("TRN2", target_bir_lowering=False, num_devices=1)
    arrays, args = {}, []
    for name in _INS:
        a = _np.ascontiguousarray(inputs[name])
        arrays[f"in_{name}_dram"] = a
        args.append(nc.dram_tensor(f"in_{name}_dram", a.shape, _mybir.dt.from_np(a.dtype), kind="ExternalInput").ap())
    for i, (shape, dtype) in enumerate(_OUTS):
        dt = _mybir.dt.from_np(_np.dtype(dtype))
        args.append(nc.dram_tensor(f"out_{i}_dram", shape, dt, kind="ExternalOutput").ap())
    gnn_resnorm(nc, *args)
    r = _run(nc, [arrays], core_ids=[0])
    got = tuple(r.results[0][f"out_{i}_dram"] for i in range(len(_OUTS)))
    return got[0]
```

```python
from contextlib import ExitStack

import concourse.bass as bass
from concourse import mybir
from concourse.alu_op_type import AluOpType as ALU

P = 128
F32 = mybir.dt.float32
F32R = mybir.dt.float32r
I32 = mybir.dt.int32
ACT = mybir.ActivationFunctionType
AX_X = mybir.AxisListType.X

BN_EPS = 1e-5
LN_EPS = 1e-5
FAR = 1024



def gnn_resnorm(nc, x, src, dst, edge, w1, b1, w2, b2, gamma, beta, out):
    N, D = x.shape
    E = src.shape[0]
    KB = D // P
    PAIR = 2 * P
    PAIRS = N // PAIR
    REST = N - PAIRS * PAIR
    TILES = 2 * PAIRS + 1
    GRAN = 32
    GRIDS = P // GRAN
    CH = -(-E // P)
    LAST_ROW = E - P
    TN = 80
    SPILLED = 16
    LOOPED = PAIRS - 1
    KEPT = LOOPED - SPILLED
    assert 0 < REST <= P and REST % 2 == 0 and TILES <= TN and CH < P
    assert KEPT > SPILLED
    chunks_of = [-(-(E - GRAN * r) // P) for r in range(GRIDS)]
    assert chunks_of == [CH] + [CH - 1] * (GRIDS - 1)
    last_new = [E - GRAN * r - (chunks_of[r] - 1) * P for r in range(GRIDS)]
    COLS = GRIDS * CH
    NOTHING = 2 * CH - 1
    SHIFT = GRIDS.bit_length() - 1
    ROUND = 2
    MRING = 2 * ROUND
    AHEAD = 4
    ERING = AHEAD * ROUND
    TP = TN // 2
    TPR = TP + 8
    TRING = 4

    h2_dram = nc.dram_tensor("h2_spilled", [SPILLED * PAIR, D], F32, kind="Internal").ap()

    with ExitStack() as ctx:
        def sb(name, shape, dt=F32):
            return ctx.enter_context(nc.sbuf_tensor(name, shape, dt))

        def pb(name, shape):
            return ctx.enter_context(nc.psum_tensor(name, shape, F32))

        def sem(name):
            return ctx.enter_context(nc.semaphore(name))

        store = sb("store", [P, 2 * (KEPT + 1) + 1, D])
        ident = sb("ident", [P, P])
        ones = sb("ones", [P, P])
        acc1 = sb("acc1", [P, D])
        acc2 = sb("acc2", [P, D])
        iota_row = sb("iota_row", [P, P])
        tile_off = sb("tile_off", [P, TN])
        dst_col = sb("dst_col", [P, COLS])
        src_col = sb("src_col", [P, COLS], I32)
        idx = [sb(f"idx{s}", [P, 1], I32) for s in range(ERING)]
        rel = sb("rel", [P, ERING])
        table = sb("table", [1, 4, TN], I32)
        b1_col = sb("b1_col", [P, KB])
        gamma_col = sb("gamma_col", [P, KB])
        beta_col = sb("beta_col", [P, KB])
        main = ExitStack()

        def sbm(name, shape, dt=F32):
            return main.enter_context(nc.sbuf_tensor(name, shape, dt))

        w_hi = [sbm(f"w{i}_hi", [P, KB, D], F32R) for i in (1, 2)]
        w_lo = [sbm(f"w{i}_lo", [P, KB, D], F32R) for i in (1, 2)]
        hT_hi = sbm("hT_hi", [P, KB, PAIR], F32R)
        hT_lo = sbm("hT_lo", [P, KB, PAIR], F32R)
        zT_hi = sbm("zT_hi", [P, KB, PAIR], F32R)
        zT_lo = sbm("zT_lo", [P, KB, PAIR], F32R)
        z_full = sbm("z_full", [P, 2, PAIR])
        x_in = sbm("x_in", [P, 2, 2, D])
        h = sbm("h", [P, 2, D])
        mess = sbm("mess", [P, ERING, D])
        m_hi = sbm("m_hi", [P, MRING, D], F32R)
        m_lo = sbm("m_lo", [P, MRING, D], F32R)
        onehot = sbm("onehot", [P, MRING, P], F32R)
        sq = sbm("sq", [P, 2, D])
        b2_all = sbm("b2_all", [P, D])
        w_raw = store[:, 0:2 * KB, :].rearrange("p (i k) d -> p i k d", i=2)
        st = [2 * KB]

        def scratch(parts, cols, dt=F32):
            view = store[0:parts, st[0], 0:cols]
            st[0] += 1
            return view if dt == F32 else view.bitcast(dt)

        dst_i, src_i = (scratch(CH + 1, P, I32) for _ in range(2))
        dst_f, src_f = (scratch(CH + 1, P) for _ in range(2))
        cols = scratch(P, 2 * (CH + 1)).rearrange("p (w c) -> p w c", w=2)
        shift_ones = scratch(P, 3 * P)
        shifter = scratch(P, 3 * P)
        new_here = scratch(P, GRIDS)
        last_up = scratch(P, 1)
        last_masked = scratch(P, GRIDS)
        tile_i = scratch(CH, P, I32)
        tile_f = scratch(CH, P)
        tile_far = scratch(CH, P)
        tile_up = scratch(CH, P)
        t_max = scratch(CH, GRIDS)
        t_min = scratch(CH, GRIDS)
        gran = scratch(CH, GRIDS)
        gran_last = scratch(CH, GRIDS)
        gran_first = scratch(CH, GRIDS)
        iota_n = scratch(CH, TN)
        from_low, cover = (scratch(CH, GRIDS * TN).rearrange("c (g n) -> c g n", g=GRIDS) for _ in range(2))
        range_f, range_l = (scratch(CH, GRIDS * TN).rearrange("c (g n) -> c g n", g=GRIDS) for _ in range(2))
        nf = scratch(TN, 16)
        ni = scratch(TN, 16, I32)
        whole = scratch(TP, TPR)
        earlier = scratch(TP, TPR)
        most = scratch(1, TP)
        rounds_col = scratch(TP, 1)
        assert st[0] <= 2 * (KEPT + 1) + 1
        main.close()

        def sbt(name, shape, dt=F32):
            return ctx.enter_context(nc.sbuf_tensor(name, shape, dt))

        x_tail = sbt("x_tail", [P, TRING, 2, D])
        u_out = sbt("u_out", [P, TRING, 2, D])
        stats = sbt("stats", [P, 2, 2, 6])
        mean_var = sbt("mean_var", [P, 2, 2, 2])
        std = sbt("std", [P, TRING, 2])
        rstd = sbt("rstd", [P, TRING, 2])
        shift = sbt("shift", [P, TRING, 2])
        bn_a = sbt("bn_a", [P, D])
        row_parts = sbt("row_parts", [64, D], F32R)
        row_pick = sbt("row_pick", [64, P], F32R)
        spread = [sbt(f"spread_{n}", [P, KB, P]) for n in ("scale", "offset")]
        bn_mean = sbt("bn_mean", [P, 2 * KB])
        bn_mean_sq = sbt("bn_mean_sq", [P, KB])
        bn_var = sbt("bn_var", [P, KB])
        bn_std = sbt("bn_std", [P, KB])
        bn_rstd = sbt("bn_rstd", [P, KB])
        bn_scale = sbt("bn_scale", [P, KB])
        bn_ms = sbt("bn_ms", [P, KB])
        bn_offset = sbt("bn_offset", [P, KB])
        root_of_one = sbt("root_of_one", [P, 1])
        eps_bn = sbt("eps_bn", [P, 1])
        eps_ln = sbt("eps_ln", [P, 1])

        ps_sum = [pb(f"ps_sum{a}", [P, D]) for a in range(2)]
        ps_turn = [pb(f"ps_turn{a}", [P, KB, P]) for a in range(2)]
        ps_z = [pb(f"ps_z{a}", [P, D]) for a in range(2)]
        ps_o = [pb(f"ps_o{a}", [P, D]) for a in range(2)]
        tail_banks = [ps_sum, ps_o, ps_turn, ps_z]

        shifted_grids = ps_o[0][:, 0:(GRIDS - 1) * 2 * (CH - 2)].rearrange("p (r w c) -> p r w c", w=2, c=CH - 2)

        s_idx = sem("s_idx")
        s_fill = sem("s_fill")
        s_w = sem("s_w")
        s_bias = sem("s_bias")
        s_const = sem("s_const")
        s_set = sem("s_set")
        s_link = sem("s_link")
        s_turned = sem("s_turned")
        s_table = sem("s_table")
        s_grid0 = sem("s_grid0")
        s_shifted = sem("s_shifted")
        s_cols = sem("s_cols")
        s_pick = sem("s_pick")
        s_acc0 = sem("s_acc0")
        s_wsplit = sem("s_wsplit")
        s_wlow = sem("s_wlow")
        e_landed = [sem(f"e_landed{s}") for s in range(ERING)]
        g_landed = [sem(f"g_landed{s}") for s in range(ERING)]
        idx_copied = sem("idx_copied")
        m_hi_done = sem("m_hi_done")
        rel_done = sem("rel_done")
        m_done = sem("m_done")
        m_used = sem("m_used")
        x_landed = sem("x_landed")
        h_done = sem("h_done")
        h_turned = sem("h_turned")
        hT_hi_done = sem("hT_hi_done")
        hT_done = sem("hT_done")
        z_ready = sem("z_ready")
        z_read = sem("z_read")
        z_done = sem("z_done")
        o_ready = sem("o_ready")
        xb_done = sem("xb_done")
        sums_done = sem("sums_done")
        h2_done = sem("h2_done")
        sq_done = sem("sq_done")
        acc1_done = sem("acc1_done")
        acc_done = sem("acc_done")
        spilled = sem("spilled")
        s_tot = sem("s_tot")
        s_spread = sem("s_spread")
        s_bn = sem("s_bn")
        s_bn_act = sem("s_bn_act")
        BN_DONE = 11
        xt_landed = [sem(f"xt_landed{s}") for s in range(TRING)]
        back_landed = [sem(f"back_landed{s}") for s in range(TRING)]
        out_landed = [sem(f"out_landed{s}") for s in range(TRING)]
        pre_ready = sem("pre_ready")
        scaled = sem("scaled")
        u_done = sem("u_done")
        stat_self = sem("stat_self")
        var_done = sem("var_done")
        std_done = sem("std_done")
        rstd_done = sem("rstd_done")
        shift_done = sem("shift_done")
        norm_done = sem("norm_done")

        block = ctx.enter_context(nc.Block())

        def by_turn(eng, g, do):
            def among(low, many):
                if many == 1:
                    do(low)
                    return
                with eng.If(g % AHEAD < low + many // 2):
                    among(low, many // 2)
                with eng.Else():
                    among(low + many // 2, many // 2)
            among(0, AHEAD)

        def more_rounds(eng, g0, g1, do):
            with eng.If(g1 > g0 + 1):
                with eng.Fori(g0 + 1, g1) as g:
                    do(g)
            with eng.Else():
                eng.nop()

        def place(i):
            return PAIRS if isinstance(i, int) and i == PAIRS else PAIRS - 1 - i

        def look_up(eng, n, row, low, high):
            return eng.value_load(table[0:1, row, bass.ds(n, 1)], min_val=low, max_val=high)

        MOST = CH
        MOST_ROUNDS = MOST * TP

        def first_row(eng, n): return look_up(eng, n, 0, 0, E)
        def first_col(eng, n): return look_up(eng, n, 1, 0, COLS - 1)
        def chunks(eng, n): return look_up(eng, n, 2, 1, MOST)
        def rounds_before(eng, p): return look_up(eng, p, 3, 0, MOST_ROUNDS)
        def rounds(eng, p): return rounds_before(eng, p), rounds_before(eng, p + 1)

        GROUPS = (LOOPED + 2) // TRING
        assert (LOOPED + 2) % TRING == 0
        starts = sorted({0, 1, SPILLED // TRING, -(-SPILLED // TRING), KEPT // TRING, -(-KEPT // TRING), LOOPED // TRING, GROUPS})
        starts = sorted(set(starts) | {g - 1 for g in starts if g > 1})
        RANGES = list(zip(starts, starts[1:]))

        def lies(q, like):
            if like < KEPT:
                return 2 * q, q + KEPT if like < SPILLED else q, 2, P
            if like < LOOPED:
                return 2 * q - 2 * KEPT, q - KEPT, 2, P
            return (2 * KEPT, PAIRS - 1, 2, P) if like == LOOPED else (2 * KEPT + 2, PAIRS, 1, REST)

        def tail(eng, do):
            for lo, hi in RANGES:
                if hi - lo == 1:
                    for t in range(TRING):
                        do(lo, t, lo * TRING + t, lo * TRING + t)
                else:
                    with eng.Fori(lo, hi) as j:
                        for t in range(TRING):
                            do(j, t, j * TRING + t, lo * TRING + t)

        def rows_of(array, pair):
            return rows_from(array, pair * PAIR)

        def rows_from(array, start):
            rows = array[start:start + PAIR, :] if isinstance(start, int) else array[bass.ds(start, PAIR), :]
            return rows.rearrange("(a p) d -> p a d", p=P)

        def pick(buf, slot, rows=P):
            if isinstance(slot, int):
                return buf[0:rows, slot]
            view = buf[0:rows, bass.ds(slot, 1)]
            rest = " ".join("abc"[:len(view.shape) - 2])
            return view.rearrange(f"p o {rest} -> p (o {rest[0]}) {rest[1:]}")

        @block.sync
        def _(sp):
            sp.wait_ge(s_fill, 1)
            whole_rows = (CH - 1) * P
            for there, here in ((dst, dst_i), (src, src_i)):
                sp.dma_start(here[0:CH - 1, :], there[0:whole_rows].rearrange("(c p) -> c p", p=P)).then_inc(s_idx, 16)
                sp.dma_start(here[CH - 1:CH, 0:E - whole_rows], there[whole_rows:E].rearrange("(c p) -> c p", c=1)).then_inc(s_idx, 16)
                sp.dma_start(here[CH:CH + 1, :], there[LAST_ROW:E].rearrange("(c p) -> c p", c=1)).then_inc(s_idx, 16)
            sp.dma_start(w_raw[:, 0], w1.rearrange("(k p) d -> p k d", p=P)).then_inc(s_w, 16)
            sp.dma_start(w_raw[:, 1], w2.rearrange("(k p) d -> p k d", p=P)).then_inc(s_w, 16)
            sp.wait_ge(s_table, 1)

            def wait_for(held, held_value, semaphore, value):
                sp.wait_ge(held, held_value)
                sp.wait_ge(semaphore, value)

            def load_edges(p):
                rows0 = [first_row(sp, 2 * place(p) + a) for a in range(2)]
                g0, g1 = rounds(sp, p)
                with sp.Fori(g0, g1) as g:
                    rows, free = [], []
                    for t in range(ROUND):
                        row = rows0[t] + (g - g0) * P
                        over = row > LAST_ROW
                        rows.append(sp.snap((row - over * (row - LAST_ROW)).with_bounds(min_val=0, max_val=LAST_ROW)))
                        free.append(sp.snap(g * ROUND + t + 1))

                    def load(turn):
                        for t in range(ROUND):
                            s = turn * ROUND + t
                            wait_for(s_table, 1, m_done, free[t])
                            sp.dma_start(mess[:, s, :], edge[bass.ds(rows[t], P), :]).then_inc(e_landed[s], 16)
                    by_turn(sp, g, load)

            LATER = 8
            assert LATER + SPILLED <= min(PAIRS, KEPT + 2)
            with sp.Fori(0, LATER) as p:
                load_edges(p)
            with sp.Fori(LATER, LATER + SPILLED) as p:
                i = p - LATER
                start, made = sp.snap(i * PAIR), sp.snap(2 * i + 4)
                wait_for(s_table, 1, h2_done, made)
                sp.dma_start(rows_from(h2_dram, start), store[:, bass.ds(2 * i, 2), :]).then_inc(spilled, 16)
                load_edges(p)
            with sp.Fori(LATER + SPILLED, PAIRS) as p:
                load_edges(p)
            load_edges(PAIRS)

            def store_out(j, t, q, like):
                slot, pair, tiles, rows = lies(q, like)
                if isinstance(j, int):
                    start = place(pair) * PAIR
                else:
                    first = lies(t, like)[1]
                    start = sp.snap(j * (-TRING * PAIR) + (PAIRS - 1 - first) * PAIR)
                before = j * 16 if isinstance(j, int) else sp.snap(j * 16)
                if TRING <= like < SPILLED:
                    wait_for(s_bn, BN_DONE, back_landed[t], before)
                wait_for(s_bn, BN_DONE, norm_done, q + 1)
                if rows == P:
                    sp.dma_start(rows_from(out, start), u_out[:, t, :, :]).then_inc(out_landed[t], 16)
                else:
                    sp.dma_start(out[N - REST:N, :], u_out[0:REST, t, 0, :]).then_inc(out_landed[t], 16)
                if like < SPILLED:
                    start = q * PAIR if isinstance(q, int) else sp.snap(q * PAIR)
                    wait_for(s_bn, BN_DONE, u_done, q + 1 + TRING)
                    sp.dma_start(store[:, 2 * q:2 * q + 2, :] if isinstance(q, int) else store[:, bass.ds(2 * q, 2), :],
                                 rows_from(h2_dram, start)).then_inc(back_landed[t], 16)
            tail(sp, store_out)
            for t in range(TRING):
                sp.wait_ge(out_landed[t], 16 * GROUPS)

        @block.gpsimd
        def _(pool):
            nc.gpsimd.memset(dst_i, -1)
            nc.gpsimd.memset(src_i, 0).then_inc(s_fill, 1)
            nc.gpsimd.memset(shift_ones, 1.0)
            nc.gpsimd.memset(ones[:], 1.0).then_inc(s_const, 1)
            pool.wait_ge(s_const, 1)
            nc.gpsimd.affine_select(out=ident[:], in_=ones[:], compare_op=ALU.is_equal, fill=0.0, base=0,
                                    pattern=[[1, P]], channel_multiplier=-1)
            assert TP == PAIRS + 1
            nc.gpsimd.affine_select(out=whole, in_=ones[0:TP, 0:TPR], compare_op=ALU.is_ge, fill=0.0, base=-PAIRS,
                                    pattern=[[1, TPR]], channel_multiplier=1).then_inc(s_const, 1)
            pool.wait_ge(s_const, 2)
            nc.gpsimd.affine_select(out=earlier, in_=whole, compare_op=ALU.is_gt, fill=0.0, base=PAIRS * TP - PAIRS,
                                    pattern=[[1, TPR]], channel_multiplier=-TP)
            nc.gpsimd.affine_select(out=shifter, in_=shift_ones, compare_op=ALU.is_equal, fill=0.0, base=-P,
                                    pattern=[[1, 3 * P]], channel_multiplier=-1)
            for r in range(GRIDS):
                nc.gpsimd.affine_select(out=new_here[:, r:r + 1], in_=ones[:, 0:1], compare_op=ALU.is_ge, fill=0.0,
                                        base=last_new[r] - P, pattern=[[1, 1]], channel_multiplier=1)
            nc.gpsimd.iota(iota_row[:], pattern=[[1, P]], base=0, channel_multiplier=0,
                           allow_small_or_imprecise_dtypes=True)
            nc.gpsimd.iota(iota_n, pattern=[[1, TN]], base=0, channel_multiplier=0,
                           allow_small_or_imprecise_dtypes=True)
            nc.gpsimd.iota(tile_off[:], pattern=[[P, TN]], base=0, channel_multiplier=0,
                           allow_small_or_imprecise_dtypes=True)
            nc.gpsimd.iota(gran, pattern=[[1, GRIDS]], base=0, channel_multiplier=GRIDS,
                           allow_small_or_imprecise_dtypes=True).then_inc(s_const, 1)
            nc.gpsimd.memset(acc1[:], 0.0)
            nc.gpsimd.memset(acc2[:], 0.0).then_inc(s_acc0, 1)
            pool.wait_ge(s_acc0, 1)

            def gathers(p):
                tiles = [2 * place(p), 2 * place(p) + 1]
                cols0 = [first_col(pool, n) for n in tiles]
                counts = [chunks(pool, n) for n in tiles]
                g0, g1 = rounds(pool, p)
                with pool.Fori(g0, g1) as g:
                    def gather(turn):
                        for t in range(ROUND):
                            s = turn * ROUND + t
                            beyond = g - g0 - counts[t] > -1
                            col = cols0[t] + (g - g0)
                            col = (col + beyond * (NOTHING - col)).with_bounds(min_val=0, max_val=COLS - 1)
                            step = g * ROUND + t
                            pool.wait_ge(m_done, step + 1)
                            pool.wait_ge(e_landed[s], (g // AHEAD) * 16 + 16)
                            nc.gpsimd.tensor_copy(idx[s][:], src_col[:, bass.ds(col, 1)]).then_inc(idx_copied, 1)
                            nc.gpsimd.tensor_tensor(rel[:, s:s + 1], dst_col[:, bass.ds(col, 1)], tile_off[:, bass.ds(tiles[t], 1)], ALU.subtract).then_inc(rel_done, 1)
                            pool.wait_ge(s_cols, 1)
                            pool.wait_ge(idx_copied, step + 1)
                            nc.gpsimd.indirect_dma_start(
                                out=mess[:, s, :], out_offset=None, in_=x,
                                in_offset=bass.IndirectOffsetOnAxis(ap=idx[s][:, 0:1], axis=0),
                                compute_op=ALU.add,
                            ).then_inc(g_landed[s], 16)
                    by_turn(pool, g, gather)

            def add_up(n, a, slot, rows):
                pool.wait_ge(sq_done, n + 1)
                pool.wait_ge(acc_done, n + 2)
                nc.gpsimd.tensor_tensor(acc2[0:rows, :], acc2[0:rows, :], sq[0:rows, a, :], ALU.add).then_inc(acc_done, 1)

            pool.sem_inc(acc_done, 2)
            pool.wait_ge(s_table, 1)
            pool.wait_ge(s_cols, 1)
            with pool.Fori(0, 3) as p:
                gathers(p)

            def body(i, slot_before):
                if slot_before is not None:
                    for a in range(2):
                        add_up(2 * i - 2 + a, a, slot_before + a, P)
                gathers(i + 3)
            body(0, None)
            with pool.Fori(1, KEPT + 1) as i:
                body(i, 2 * i - 2)
            with pool.Fori(KEPT + 1, PAIRS - 3) as i:
                body(i, 2 * i - 2 - 2 * KEPT)
            for i in range(PAIRS - 3, PAIRS):
                for a in range(2):
                    add_up(2 * i - 2 + a, a, 2 * i - 2 - 2 * KEPT + a, P)
                if i == PAIRS - 3:
                    gathers(PAIRS)
            for a in range(2):
                add_up(2 * PAIRS - 2 + a, a, 2 * KEPT + a, P)
            add_up(TILES - 1, 0, 2 * KEPT + 2, REST)

            pool.wait_ge(s_bn_act, 2)

            def scale(slot):
                for a in range(2):
                    s = slot + a
                    h2 = pick(store, s)
                    last = nc.gpsimd.tensor_tensor(h2, h2, bn_a[:], ALU.mult)
                last.then_inc(scaled, 1)
            with pool.Fori(0, KEPT) as q:
                scale(2 * q)
            with pool.Fori(0, SPILLED // TRING) as j:
                for t in range(TRING):
                    pool.wait_ge(back_landed[t], j * 16 + 16)
                    scale((j * TRING + t) * 2)
            for q in range(SPILLED - SPILLED % TRING, SPILLED):
                pool.wait_ge(back_landed[q % TRING], q // TRING * 16 + 16)
                scale(2 * q)
            scale(2 * KEPT)
            h2 = store[0:REST, 2 * KEPT + 2, :]
            nc.gpsimd.tensor_tensor(h2, h2, bn_a[0:REST, :], ALU.mult).then_inc(scaled, 1)

        @block.scalar
        def _(act):
            act.dma_start(b1_col[:], b1.rearrange("(k p) -> p k", p=P), allow_slow_non_contiguous=True).then_inc(s_bias, 16)
            act.dma_start(b2_all[:], b2.rearrange("(o d) -> o d", o=1).broadcast_to([P, D])).then_inc(s_bias, 16)
            act.dma_start(gamma_col[:], gamma.rearrange("(k p) -> p k", p=P), allow_slow_non_contiguous=True).then_inc(s_bias, 16)
            act.dma_start(beta_col[:], beta.rearrange("(k p) -> p k", p=P), allow_slow_non_contiguous=True).then_inc(s_bias, 16)
            act.sem_inc(z_read, 2)
            act.wait_ge(s_w, 32)
            for w in range(2):
                nc.scalar.copy(w_hi[w][:], w_raw[:, w]).then_inc(s_wsplit, 1)

            act.dma_start(x_in[:, 0, :, :], rows_of(x, place(0))).then_inc(x_landed, 16)
            act.wait_ge(x_landed, 16)
            act.dma_start(x_in[:, 1, :, :], rows_of(x, place(1))).then_inc(x_landed, 16)

            def hT_high(n, a, rows):
                act.wait_ge(h_turned, n + 3)
                nc.scalar.copy(hT_hi[:, :, a * P:a * P + rows], ps_turn[a][:, :, 0:rows]).then_inc(hT_hi_done, 1)

            def m_high(g_range):
                g0, g1 = g_range

                def one(g, base, free):
                    def high(turn):
                        for t in range(ROUND):
                            s = turn * ROUND + t
                            act.wait_ge(g_landed[s], (g // AHEAD) * 16 + 16)
                            act.wait_ge(m_used, free(t))
                            nc.scalar.activation(m_hi[:, base + t, :], mess[:, s, :], ACT.Relu).then_inc(m_hi_done, 1)
                    by_turn(act, g, high)
                one(g0, 0, lambda t: g0 * ROUND + ROUND)

                def further(g):
                    third = g - g0 > 1
                    one(g, ROUND, lambda t: g * ROUND + third * (t + 1))
                more_rounds(act, g0, g1, further)

            act.wait_ge(s_table, 1)
            m_high(rounds(act, 0))
            act.wait_ge(s_bias, 64)
            for a in range(2):
                hT_high(a, a, P)
            m_high(rounds(act, 1))

            def z_high(i, cols, blocks=range(KB)):
                for f in blocks:
                    act.wait_ge(z_ready, 4 * i + f + 1)
                    act.wait_ge(z_done, 4 * i + f + 1)
                    nc.scalar.activation(z_full[:, f % 2, 0:cols], ps_z[f % 2][:, 0:cols], ACT.Relu, bias=b1_col[:, f:f + 1])
                    nc.scalar.activation(zT_hi[:, f, 0:cols], ps_z[f % 2][:, 0:cols], ACT.Relu, bias=b1_col[:, f:f + 1]).then_inc(z_read, 1)

            def squares(n, a, slot, rows):
                act.wait_ge(h2_done, n + 3)
                act.wait_ge(acc_done, n + 1)
                h2 = pick(store, slot, rows)
                nc.scalar.activation(sq[0:rows, a, :], h2, ACT.Square).then_inc(sq_done, 1)

            def body(i, slot_before):
                z_high(i, PAIR, (0,))
                if slot_before is not None:
                    act.wait_ge(h2_done, 2 * i + 2)
                    act.dma_start(pick(x_in, (i + 1) % 2), rows_of(x, place(i + 1))).then_inc(x_landed, 16)
                z_high(i, PAIR, (1,))
                if slot_before is not None:
                    for a in range(2):
                        squares(2 * i - 2 + a, a, slot_before + a, P)
                next_rounds = rounds(act, i + 2)
                z_high(i, PAIR, (2, 3))
                m_high(next_rounds)
                for a in range(2):
                    hT_high(2 * i + 2 + a, a, P)
            body(0, None)
            with act.Fori(1, KEPT + 1) as i:
                body(i, 2 * i - 2)
            with act.Fori(KEPT + 1, LOOPED) as i:
                body(i, 2 * i - 2 - 2 * KEPT)
            i = PAIRS - 1
            z_high(i, PAIR, (0,))
            act.wait_ge(h2_done, 2 * i + 2)
            act.dma_start(x_in[0:REST, PAIRS % 2, 0, :], x[N - REST:N, :]).then_inc(x_landed, 16)
            z_high(i, PAIR, (1,))
            for a in range(2):
                squares(2 * i - 2 + a, a, 2 * i - 2 - 2 * KEPT + a, P)
            z_high(i, PAIR, (2, 3))
            hT_high(2 * i + 2, 0, REST)
            for a in range(2):
                squares(2 * i + a, a, 2 * KEPT + a, P)
            z_high(PAIRS, REST)
            squares(TILES - 1, 0, 2 * KEPT + 2, REST)

            def load_tail(q, like):
                t, (slot, pair, tiles, rows) = like % TRING, lies(q, like)
                if rows == P:
                    act.dma_start(x_tail[:, t, :, :], rows_of(x, place(pair))).then_inc(xt_landed[t], 16)
                else:
                    act.dma_start(x_tail[0:REST, t, 0, :], x[N - REST:N, :]).then_inc(xt_landed[t], 16)

            act.wait_ge(acc_done, TILES + 2)
            act.wait_ge(o_ready, TILES)
            for q in range(TRING):
                load_tail(q, q)
            nc.scalar.activation(root_of_one[:], ones[:, 0:1], ACT.Sqrt)
            act.wait_ge(s_bn, 3)
            nc.scalar.activation(bn_std[:], bn_var[:], ACT.Sqrt, bias=eps_bn[:]).then_inc(s_bn_act, 1)
            act.wait_ge(s_spread, 1)
            nc.scalar.copy(bn_a[:], ps_z[0][:]).then_inc(s_bn_act, 1)

            def finish(j, t, q, like):
                slot, pair, tiles, rows = lies(q, like)
                if like < LOOPED + 2 - TRING:
                    act.wait_ge(pre_ready, q + 1)
                    load_tail(q + TRING, like + TRING)
                act.wait_ge(var_done, q + 1)
                nc.scalar.activation(std[0:rows, t, 0:tiles], mean_var[0:rows, t % 2, 0:tiles, 1], ACT.Sqrt, bias=eps_ln[0:rows, :]).then_inc(std_done, 1)
                act.wait_ge(shift_done, q + 1)
                for a in range(tiles):
                    u = u_out[0:rows, t, a, :]
                    last = nc.scalar.activation(u, u, ACT.Identity, bias=shift[0:rows, t, a:a + 1], scale=rstd[0:rows, t, a:a + 1])
                last.then_inc(norm_done, 1)
            tail(act, finish)

        @block.tensor
        def _(pe):
            mm = nc.tensor.matmul
            pe.sem_inc(m_used, ROUND)
            pe.sem_inc(h_turned, 2)
            pe.wait_ge(s_const, 3)
            pe.wait_ge(s_set, 1)
            nc.tensor.transpose(ps_turn[0][:, 0, 0:CH + 1], dst_f, ident[0:CH + 1, 0:CH + 1])
            nc.tensor.transpose(ps_turn[0][:, 1, 0:CH + 1], src_f, ident[0:CH + 1, 0:CH + 1]).then_inc(s_turned, 1)
            pe.wait_ge(s_grid0, 1)
            for r in range(1, GRIDS):
                part = shifted_grids[:, r - 1, :, :]
                mm(part, shifter[:, P + GRAN * r:2 * P + GRAN * r], cols[:, :, 0:CH - 2], start=True, stop=False)
                t = mm(part, shifter[:, GRAN * r:P + GRAN * r], cols[:, :, 1:CH - 1], start=False, stop=True)
            t.then_inc(s_shifted, 1)
            pe.wait_ge(s_set, 2)
            nc.tensor.transpose(ps_turn[1][0:TN, 0, 0:CH], range_f[:, GRIDS - 1, :], ident[0:CH, 0:CH])
            nc.tensor.transpose(ps_turn[1][0:TN, 1, 0:CH], range_l[:, GRIDS - 1, :], ident[0:CH, 0:CH]).then_inc(s_turned, 1)
            pe.wait_ge(s_set, 3)
            mm(ps_z[0][0:1, 0:TN], nf[:, 8:9], ident[0:TN, 0:TN], start=True, stop=True)
            mm(ps_z[0][0:1, TN:2 * TN], nf[:, 9:10], ident[0:TN, 0:TN], start=True, stop=True)
            mm(ps_z[0][0:1, 2 * TN:3 * TN], nf[:, 10:11], ident[0:TN, 0:TN], start=True, stop=True).then_inc(s_turned, 1)
            pe.wait_ge(s_set, 4)
            mm(ps_z[1][0:TP, 0:1], most, ones[0:1, 0:1], start=True, stop=True).then_inc(s_turned, 1)
            pe.wait_ge(s_set, 5)
            mm(ps_z[1][0:1, 0:TPR], rounds_col, earlier, start=True, stop=True).then_inc(s_turned, 1)
            pe.wait_ge(s_table, 1)

            def pair_sums(p):
                g0, g1 = rounds(pe, p)
                pe.wait_ge(h_done, 2 * p + 2)

                def one(g, base):
                    for t in range(ROUND):
                        pe.wait_ge(m_done, g * ROUND + t + ERING + 1)
                        mm(ps_sum[t][:], onehot[:, base + t, :], m_hi[:, base + t, :], start=base == 0, stop=False, skip_group_check=True)
                        mm(ps_sum[t][:], onehot[:, base + t, :], m_lo[:, base + t, :], start=False, stop=True,
                           skip_group_check=True).then_inc(m_used, 1)
                one(g0, 0)
                more_rounds(pe, g0, g1, lambda g: one(g, ROUND))

            def turn(n, a, rows):
                pe.wait_ge(h_done, n + 3)
                pe.wait_ge(hT_done, n + 1)
                for k in range(KB):
                    t = nc.tensor.transpose(ps_turn[a][:, k, 0:rows], h[0:rows, a, k * P:(k + 1) * P], ident[0:rows, 0:rows])
                t.then_inc(h_turned, 1)

            def layer1(i, cols, tiles_done):
                pe.wait_ge(hT_hi_done, tiles_done)
                for f in range(KB):
                    pe.wait_ge(z_read, 4 * i + f + 1)
                    out_ = ps_z[f % 2][:, 0:cols]
                    parts = [(w_hi[0], hT_hi), (w_lo[0], hT_hi), (w_hi[0], hT_lo)]
                    for m in range(3 * KB):
                        w, r = parts[m // KB]
                        if f == 0 and m == 2 * KB:
                            pe.wait_ge(hT_done, tiles_done + 2)
                        t = mm(out_, w[:, m % KB, f * P:(f + 1) * P], r[:, m % KB, 0:cols], start=(m == 0), stop=(m == 3 * KB - 1))
                        if f == 0 and m == 0:
                            t.then_inc(sums_done, 1)
                    t.then_inc(z_ready, 1)

            def layer2(i, n, a):
                pe.wait_ge(h2_done, n + 1)
                for f in range(KB):
                    pe.wait_ge(z_done, 4 * i + f + 3)
                    for m, (l, w) in enumerate(((zT_hi, w_hi[1]), (zT_hi, w_lo[1]), (zT_lo, w_hi[1]))):
                        t = mm(ps_o[a][:], l[:, f, a * P:(a + 1) * P], w[:, f, :], start=(f == 0 and m == 0), stop=(f == KB - 1 and m == 2))
                t.then_inc(o_ready, 1)

            pe.wait_ge(s_wlow, 2)
            pair_sums(0)
            for a in range(2):
                turn(a, a, P)
            with pe.Fori(0, LOOPED) as i:
                pair_sums(i + 1)
                layer1(i, PAIR, 2 * i + 2)
                layer2(i, 2 * i, 0)
                for a in range(2):
                    turn(2 * i + 2 + a, a, P)
                layer2(i, 2 * i + 1, 1)
            i = PAIRS - 1
            pair_sums(PAIRS)
            layer1(i, PAIR, 2 * i + 2)
            layer2(i, 2 * i, 0)
            turn(TILES - 1, 0, REST)
            layer2(i, 2 * i + 1, 1)
            layer1(PAIRS, REST, TILES)
            layer2(PAIRS, TILES - 1, 0)

            for w, (acc, summed, tiles) in enumerate(((acc1, acc1_done, TILES + 1), (acc2, acc_done, TILES + 2))):
                pe.wait_ge(summed, tiles)
                for k in range(KB):
                    t = mm(ps_z[0][:, w * KB + k:w * KB + k + 1], acc[:, k * P:(k + 1) * P], ones[:, 0:1], start=True, stop=True)
            t.then_inc(s_tot, 1)
            for w, made in enumerate((6, 9)):
                pe.wait_ge(s_bn, made)
                for k in range(KB):
                    t = mm(ps_z[w][:, k * P:(k + 1) * P], ones[:], spread[w][:, k, :], start=True, stop=True)
                t.then_inc(s_spread, 1)

            def pre(j, t, q, like):
                slot, pair, tiles, rows = lies(q, like)
                pe.wait_ge(xt_landed[t], j * 16 + 16)
                pe.wait_ge(u_done, q + 1)
                for a in range(tiles):
                    bank = tail_banks[t][a][:] if tail_banks[t] is not ps_turn else tail_banks[t][a][:].rearrange("p k c -> p (k c)")
                    mm(bank, row_pick[:], row_parts[:], start=True, stop=False, skip_group_check=True)
                    last = mm(bank, ident[0:rows, :], x_tail[0:rows, t, a, :], start=False, stop=True, skip_group_check=True)
                last.then_inc(pre_ready, 1)
            pe.wait_ge(s_bn, BN_DONE)
            pe.wait_ge(s_bn_act, 2)
            tail(pe, pre)

        @block.vector
        def _(dve):
            v = nc.vector
            dve.sem_inc(m_done, ERING)
            dve.sem_inc(acc1_done, 1)
            dve.sem_inc(h_done, 2)
            dve.sem_inc(hT_done, 2)
            dve.sem_inc(z_done, 2)
            dve.sem_inc(h2_done, 2)
            dve.sem_inc(u_done, TRING)
            chain = [0]
            def link(ins):
                chain[0] += 1
                ins.then_inc(s_link, 1)
                dve.wait_ge(s_link, chain[0])

            dve.wait_ge(s_idx, 16 * 6)
            v.tensor_copy(dst_f, dst_i)
            v.tensor_copy(src_f, src_i).then_inc(s_set, 1)
            link(v.tensor_scalar(tile_i, dst_i[0:CH, :], 7, None, ALU.arith_shift_right))
            link(v.tensor_copy(tile_f, tile_i))
            link(v.tensor_scalar(tile_far, tile_f, 0.0, float(FAR), ALU.is_lt, ALU.mult))
            link(v.tensor_tensor(tile_up, tile_far, tile_f, ALU.add))
            v.tensor_reduce(t_max, tile_f.rearrange("c (g e) -> c g e", g=GRIDS), AX_X, ALU.max)
            link(v.tensor_reduce(t_min, tile_up.rearrange("c (g e) -> c g e", g=GRIDS), AX_X, ALU.min))
            dve.wait_ge(s_turned, 1)
            v.tensor_copy(cols, ps_turn[0][:, 0:2, 0:CH + 1]).then_inc(s_grid0, 1)
            dve.wait_ge(s_const, 3)
            v.tensor_scalar(gran_last, gran, 1.0, None, ALU.add)
            v.tensor_scalar(gran_first, gran, -1.0, float(FAR), ALU.mult, ALU.add)
            for g in range(GRIDS):
                last = v.tensor_scalar(from_low[:, g, :], iota_n, t_min[:, g:g + 1], None, ALU.is_ge)
            link(last)
            for g in range(GRIDS):
                last = v.scalar_tensor_tensor(cover[:, g, :], iota_n, t_max[:, g:g + 1], from_low[:, g, :], ALU.is_le, ALU.mult)
            link(last)
            for g in range(GRIDS):
                for range_, mark in ((range_f, gran_first), (range_l, gran_last)):
                    if g == 0:
                        last = v.tensor_scalar(range_[:, 0, :], cover[:, 0, :], mark[:, 0:1], None, ALU.mult)
                    else:
                        last = v.scalar_tensor_tensor(range_[:, g, :], cover[:, g, :], mark[:, g:g + 1], range_[:, g - 1, :], ALU.mult, ALU.max)
                if g < GRIDS - 1:
                    link(last)
            last.then_inc(s_set, 1)
            dst_at, src_at = (col[:, :].rearrange("p (r c) -> p r c", r=GRIDS) for col in (dst_col, src_col))
            link(v.tensor_scalar(last_up, cols[:, 0, CH:CH + 1], 1.0, None, ALU.add))
            link(v.tensor_scalar(last_masked, new_here, last_up, None, ALU.mult))
            v.memset(dst_at[:, 1:GRIDS, CH - 1:CH], -1.0)
            v.memset(src_at[:, 1:GRIDS, CH - 1:CH], 0)
            v.tensor_copy(dst_at[:, 0, 0:CH - 1], cols[:, 0, 0:CH - 1])
            v.tensor_copy(src_at[:, 0, 0:CH - 1], cols[:, 1, 0:CH - 1])
            for r in range(GRIDS):
                at = CH - 1 if r == 0 else CH - 2
                v.tensor_scalar(dst_at[:, r, at:at + 1], last_masked[:, r:r + 1], -1.0, None, ALU.add)
                v.tensor_copy(src_at[:, r, at:at + 1], cols[:, 1, CH:CH + 1])
            dve.wait_ge(s_shifted, 1)
            v.tensor_copy(dst_at[:, 1:GRIDS, 0:CH - 2], shifted_grids[:, :, 0, :])
            v.tensor_copy(src_at[:, 1:GRIDS, 0:CH - 2], shifted_grids[:, :, 1, :]).then_inc(s_cols, 1)
            dve.wait_ge(s_turned, 2)
            v.tensor_reduce(nf[:, 0:1], ps_turn[1][0:TN, 0, 0:CH], AX_X, ALU.max)
            link(v.tensor_reduce(nf[:, 1:2], ps_turn[1][0:TN, 1, 0:CH], AX_X, ALU.max))
            v.tensor_scalar(nf[:, 2:3], nf[:, 1:2], 1.0, None, ALU.is_ge)
            v.tensor_scalar(nf[:, 3:4], nf[:, 0:1], -1.0, float(FAR), ALU.mult, ALU.add)
            link(v.tensor_scalar(nf[:, 4:5], nf[:, 1:2], -1.0, 0.0, ALU.add, ALU.max))
            link(v.tensor_tensor(nf[:, 5:6], nf[:, 3:4], nf[:, 2:3], ALU.mult))
            link(v.tensor_tensor(nf[:, 6:7], nf[:, 4:5], nf[:, 5:6], ALU.subtract))
            v.tensor_copy(ni[:, 0:1], nf[:, 6:7])
            link(v.tensor_copy(ni[:, 1:2], nf[:, 5:6]))
            v.tensor_scalar(ni[:, 2:4], ni[:, 0:2], SHIFT, None, ALU.arith_shift_right)
            link(v.tensor_scalar(ni[:, 4:5], ni[:, 1:2], GRIDS - 1, None, ALU.bitwise_and))
            link(v.tensor_copy(nf[:, 11:14], ni[:, 2:5]))
            v.tensor_scalar(nf[:, 8:9], nf[:, 5:6], float(GRAN), None, ALU.mult)
            v.tensor_scalar(nf[:, 10:11], nf[:, 11:12], 1.0, None, ALU.add)
            v.scalar_tensor_tensor(nf[:, 9:10], nf[:, 13:14], float(CH), nf[:, 12:13], ALU.mult, ALU.add).then_inc(s_set, 1)
            dve.wait_ge(s_turned, 3)
            v.tensor_copy(table[0:1, 0:3, :].rearrange("o r n -> o (r n)"), ps_z[0][0:1, 0:3 * TN])
            v.tensor_reduce(most, ps_z[0][0:1, 2 * TN:3 * TN].rearrange("o (p a) -> o p a", a=2), AX_X, ALU.max).then_inc(s_set, 1)
            dve.wait_ge(s_turned, 4)
            v.tensor_copy(rounds_col, ps_z[1][0:TP, 0:1]).then_inc(s_set, 1)
            dve.wait_ge(s_turned, 5)
            v.tensor_copy(table[0:1, 3, 0:TPR], ps_z[1][0:1, 0:TPR]).then_inc(s_table, 1)
            for w in range(2):
                dve.wait_ge(s_wsplit, w + 1)
                v.tensor_tensor(w_lo[w][:], w_raw[:, w], w_hi[w][:].bitcast(F32), ALU.subtract).then_inc(s_wlow, 1)
            dve.wait_ge(s_wlow, 2)

            def m_parts(g_range):
                g0, g1 = g_range

                def one(g, base):
                    for t in range(ROUND):
                        slot = (g % AHEAD) * ROUND + t
                        dve.wait_ge(m_hi_done, g * ROUND + t + 1)
                        v.scalar_tensor_tensor(m_lo[:, base + t, :], pick(mess, slot), 0.0, m_hi[:, base + t, :].bitcast(F32), ALU.max, ALU.subtract)
                        dve.wait_ge(rel_done, g * ROUND + t + 1)
                        v.tensor_scalar(onehot[:, base + t, :], iota_row[:], rel[:, bass.ds(slot, 1)], None, ALU.is_equal).then_inc(m_done, 1)
                one(g0, 0)
                more_rounds(dve, g0, g1, lambda g: one(g, ROUND))

            def make_h(n, a, i, slot, rows):
                if not (isinstance(i, int) and i == 0):
                    dve.wait_ge(sums_done, i)
                dve.wait_ge(x_landed, 16 * i + 16)
                dve.wait_ge(h_turned, n + 1)
                v.tensor_tensor(h[0:rows, a, :], ps_sum[a][0:rows, :], pick(x_in, slot, rows)[:, a, :], ALU.add).then_inc(h_done, 1)

            def add_b2(slot, tiles, rows):
                for a in range(tiles):
                    xa = pick(x_in, slot, rows)[:, a, :]
                    last = v.tensor_tensor(xa, xa, b2_all[0:rows, :], ALU.add)
                last.then_inc(xb_done, 1)

            def hT_low(n, a, rows):
                dve.wait_ge(hT_hi_done, n + 1)
                v.tensor_tensor(hT_lo[:, :, a * P:a * P + rows], ps_turn[a][:, :, 0:rows],
                                hT_hi[:, :, a * P:a * P + rows].bitcast(F32), ALU.subtract).then_inc(hT_done, 1)

            def z_low(i, f, cols):
                dve.wait_ge(z_read, 4 * i + f + 3)
                v.tensor_tensor(zT_lo[:, f, 0:cols], z_full[:, f % 2, 0:cols], zT_hi[:, f, 0:cols].bitcast(F32), ALU.subtract).then_inc(z_done, 1)

            def make_h2(n, a, i, slot, xslot, rows):
                dve.wait_ge(o_ready, n + 1)
                dve.wait_ge(xb_done, i + 1)
                h2 = pick(store, slot, rows)
                v.tensor_tensor(h2, ps_o[a][0:rows, :], pick(x_in, xslot, rows)[:, a, :], ALU.add).then_inc(h2_done, 1)

            def add_up(n, slot, rows):
                dve.wait_ge(h2_done, n + 3)
                dve.wait_ge(acc1_done, n + 1)
                v.tensor_tensor(acc1[0:rows, :], acc1[0:rows, :], pick(store, slot, rows), ALU.add).then_inc(acc1_done, 1)

            m_parts(rounds(dve, 0))
            dve.wait_ge(m_used, rounds_before(dve, 1) * ROUND + ROUND)
            for a in range(2):
                make_h(a, a, 0, 0, P)
            for a in range(2):
                hT_low(a, a, P)
            m_parts(rounds(dve, 1))
            dve.wait_ge(s_bias, 64)
            add_b2(0, 2, P)

            def body(i, slot):
                for f in range(2):
                    z_low(i, f, PAIR)
                next_rounds = rounds(dve, i + 2)
                for f in range(2, KB):
                    z_low(i, f, PAIR)
                for a in range(2):
                    make_h(2 * i + 2 + a, a, i + 1, (i + 1) % 2, P)
                m_parts(next_rounds)
                make_h2(2 * i, 0, i, slot, i % 2, P)
                for a in range(2):
                    hT_low(2 * i + 2 + a, a, P)
                make_h2(2 * i + 1, 1, i, slot + 1, i % 2, P)
                for a in range(2):
                    add_up(2 * i + a, slot + a, P)
                add_b2((i + 1) % 2, 2, P)
            with dve.Fori(0, KEPT) as i:
                body(i, 2 * i)
            dve.wait_ge(spilled, 16 * SPILLED)
            with dve.Fori(KEPT, LOOPED) as i:
                body(i, 2 * i - 2 * KEPT)
            i = PAIRS - 1
            for f in range(KB):
                z_low(i, f, PAIR)
            make_h(TILES - 1, 0, PAIRS, PAIRS % 2, REST)
            make_h2(2 * i, 0, i, 2 * KEPT, i % 2, P)
            hT_low(TILES - 1, 0, REST)
            make_h2(2 * i + 1, 1, i, 2 * KEPT + 1, i % 2, P)
            add_b2(PAIRS % 2, 1, REST)
            for a in range(2):
                add_up(2 * i + a, 2 * KEPT + a, P)
            for f in range(KB):
                z_low(PAIRS, f, REST)
            make_h2(TILES - 1, 0, PAIRS, 2 * KEPT + 2, PAIRS % 2, REST)
            add_up(TILES - 1, 2 * KEPT + 2, REST)

            dve.wait_ge(o_ready, TILES)
            dve.wait_ge(acc_done, TILES + 2)
            v.memset(eps_bn[:], BN_EPS)
            v.memset(eps_ln[:], LN_EPS)
            v.memset(row_pick[:].bitcast(F32), 0.0).then_inc(s_pick, 1)
            dve.wait_ge(s_pick, 1)
            v.memset(row_pick[0:1, :].bitcast(F32), 1.0)
            v.memset(row_pick[32:33, :].bitcast(F32), 1.0)
            count = [0]

            def bn(ins):
                count[0] += 1
                ins.then_inc(s_bn, 1)
                dve.wait_ge(s_bn, count[0])
            dve.wait_ge(s_tot, 1)
            bn(v.tensor_scalar(bn_mean[:], ps_z[0][:, 0:2 * KB], 1.0 / N, None, ALU.mult))
            bn(v.tensor_tensor(bn_mean_sq[:], bn_mean[:, 0:KB], bn_mean[:, 0:KB], ALU.mult))
            bn(v.tensor_tensor(bn_var[:], bn_mean[:, KB:2 * KB], bn_mean_sq[:], ALU.subtract))
            dve.wait_ge(s_bn_act, 1)
            bn(v.reciprocal(bn_rstd[:], bn_std[:]))
            bn(v.tensor_tensor(bn_scale[:], bn_rstd[:], gamma_col[:], ALU.mult))
            for k in range(KB):
                last = v.tensor_scalar(spread[0][:, k, :], ident[:], bn_scale[:, k:k + 1], None, ALU.mult)
            bn(last)
            bn(v.tensor_tensor(bn_ms[:], bn_mean[:, 0:KB], bn_scale[:], ALU.mult))
            bn(v.tensor_tensor(bn_offset[:], beta_col[:], bn_ms[:], ALU.subtract))
            for k in range(KB):
                last = v.tensor_scalar(spread[1][:, k, :], ident[:], bn_offset[:, k:k + 1], None, ALU.mult)
            bn(last)
            dve.wait_ge(s_spread, 2)
            bn(v.tensor_copy(row_parts[0:64, :], ps_z[1][0:64, :]))
            bn(v.tensor_tensor(row_parts[32:64, :], ps_z[1][32:64, :], row_parts[32:64, :].bitcast(F32), ALU.subtract))
            assert count[0] == BN_DONE

            def row_scale(q, t, tiles, rows):
                dve.wait_ge(std_done, q + 1)
                v.reciprocal(rstd[0:rows, t, 0:tiles], std[0:rows, t, 0:tiles]).then_inc(rstd_done, 1)
                dve.wait_ge(rstd_done, q + 1)
                v.scalar_tensor_tensor(shift[0:rows, t, 0:tiles], mean_var[0:rows, t % 2, 0:tiles, 0], -1.0,
                                       rstd[0:rows, t, 0:tiles], ALU.mult, ALU.mult).then_inc(shift_done, 1)

            def row_stats(q, t, tiles, rows):
                dve.wait_ge(s_bn, BN_DONE)
                dve.wait_ge(stat_self, q + 1)
                for a in range(tiles):
                    last = v.bn_aggr(mean_var[0:rows, t % 2, a, :], stats[0:rows, t % 2, a, :])
                last.then_inc(var_done, 1)

            def sum_up(j, t, q, like):
                slot, pair, tiles, rows = lies(q, like)
                if like >= TRING:
                    dve.wait_ge(out_landed[t], j * 16)
                dve.wait_ge(pre_ready, q + 1)
                dve.wait_ge(scaled, q + 1)
                for a in range(tiles):
                    bank = tail_banks[t][a][0:rows, :] if tail_banks[t] is not ps_turn else tail_banks[t][a][0:rows].rearrange("p k c -> p (k c)")
                    last = v.tensor_tensor(u_out[0:rows, t, a, :], bank, pick(store, slot + a, rows), ALU.add)
                last.then_inc(u_done, 1)
                if like > 0:
                    row_stats(q - 1, (t - 1) % TRING, 2, P)
                dve.wait_ge(s_bn, BN_DONE)
                dve.wait_ge(u_done, q + 1 + TRING)
                for a in range(tiles):
                    last = v.bn_stats(stats[0:rows, t % 2, a, :], u_out[0:rows, t, a, :])
                last.then_inc(stat_self, 1)
                if like > 0:
                    row_scale(q - 1, (t - 1) % TRING, 2, P)
            tail(dve, sum_up)
            q = LOOPED + 1
            row_stats(q, q % TRING, 1, REST)
            row_scale(q, q % TRING, 1, REST)


_INS = ['x', 'src', 'dst', 'edge_attr_512', 'L0_gnn_W1', 'L0_gnn_b1', 'L0_gnn_W2', 'L0_gnn_b2', 'L0_gnn_gamma', 'L0_gnn_beta']
_OUTS = [((10000, 512), 'float32')]


def kernel(**inputs):
    import numpy as _np
    import concourse.bacc as _bacc
    from concourse import mybir as _mybir
    from concourse.bass_utils import run_bass_kernel_spmd as _run

    nc = _bacc.Bacc("TRN2", target_bir_lowering=False, num_devices=1)
    arrays, args = {}, []
    for name in _INS:
        a = _np.ascontiguousarray(inputs[name])
        arrays[f"in_{name}_dram"] = a
        args.append(nc.dram_tensor(f"in_{name}_dram", a.shape, _mybir.dt.from_np(a.dtype), kind="ExternalInput").ap())
    for i, (shape, dtype) in enumerate(_OUTS):
        dt = _mybir.dt.from_np(_np.dtype(dtype))
        args.append(nc.dram_tensor(f"out_{i}_dram", shape, dt, kind="ExternalOutput").ap())
    gnn_resnorm(nc, *args)
    r = _run(nc, [arrays], core_ids=[0])
    got = tuple(r.results[0][f"out_{i}_dram"] for i in range(len(_OUTS)))
    return got[0]
```
